# Optimizing a Trainium2 kernel written in Bass

```python
import numpy as np
import jax
import jax.numpy as jnp

def _softmax(x, axis=-1):
    return jax.nn.softmax(x, axis=axis)

def _gelu(x):
    return jax.nn.gelu(x, approximate=True)

def _silu(x):
    return jax.nn.silu(x)

def _sigmoid(x):
    return jax.nn.sigmoid(x)

def _layernorm(x, axis=-1, eps=1e-05):
    m = jnp.mean(x, axis=axis, keepdims=True)
    v = jnp.var(x, axis=axis, keepdims=True)
    return (x - m) / jnp.sqrt(v + eps)

def _scatter_add(tgt, idx, src, axis=0):
    return tgt.at[idx].add(src)

def _segment_sum(src, seg, n):
    return jax.ops.segment_sum(src, seg, n)
kernel_name = 'mk_adaln_d1_jaxref_r8_f4c3df'

def setup_inputs(seed: int=0):
    np.random.seed(seed)
    _w = jnp.asarray

    def _L0_attn_setup():
        import jax, jax.numpy as jnp
        import numpy as np
        NUM_HEADS = 16
        key = jax.random.key(seed)
        ks = jax.random.split(key, 5)
        B, N, C = (2, 256, 128)
        x = jax.random.normal(ks[0], (B, N, C), dtype=jnp.float32)
        s_in = 1.0 / np.sqrt(C)
        Wq = jax.random.normal(ks[1], (C, 2 * C), dtype=jnp.float32) * s_in
        Wk = jax.random.normal(ks[2], (C, 2 * C), dtype=jnp.float32) * s_in
        Wv = jax.random.normal(ks[3], (C, 2 * C), dtype=jnp.float32) * s_in
        Wo = jax.random.normal(ks[4], (2 * C, C), dtype=jnp.float32) * (1.0 / np.sqrt(2 * C))
        return {'x': x, 'Wq': Wq, 'Wk': Wk, 'Wv': Wv, 'Wo': Wo}
    _L0_attn_in = _L0_attn_setup()

    def _L0_ffn_setup():
        import jax, jax.numpy as jnp
        import numpy as np
        DIM = 128

        def _reference_tuple_inner(x, W_r, W_k, W_v, mu_r, mu_k):
            B, T, C = x.shape
            x_prev = jnp.concatenate([jnp.zeros((B, 1, C), x.dtype), x[:, :-1, :]], axis=1)
            xr = mu_r * x + (1.0 - mu_r) * x_prev
            xk = mu_k * x + (1.0 - mu_k) * x_prev
            r = jax.nn.sigmoid(jnp.einsum('btc,dc->btd', xr, W_r))
            k = jnp.einsum('btc,dc->btd', xk, W_k)
            k_act = jnp.square(jax.nn.relu(k))
            out = r * jnp.einsum('btc,dc->btd', k_act, W_v)
            new_state = x[:, -1, :]
            return (out, new_state)
        key = jax.random.key(seed)
        ks = jax.random.split(key, 6)
        B, T, C = (8, 256, DIM)
        x = jax.random.normal(ks[0], (B, T, C), dtype=jnp.float32)
        s = 1.0 / np.sqrt(C)
        W_r = jax.random.uniform(ks[1], (C, C), jnp.float32, -s, s)
        W_k = jax.random.uniform(ks[2], (C, C), jnp.float32, -s, s)
        W_v = jax.random.uniform(ks[3], (C, C), jnp.float32, -s, s)
        mu_r = jax.random.uniform(ks[4], (C,), jnp.float32)
        mu_k = jax.random.uniform(ks[5], (C,), jnp.float32)
        return {'x': x, 'W_r': W_r, 'W_k': W_k, 'W_v': W_v, 'mu_r': mu_r, 'mu_k': mu_k}
    _L0_ffn_in = _L0_ffn_setup()
    _L0_c = _w((lambda *s: np.random.randn(*s).astype(np.float32) * 0.05)(8, 128))
    _L0_wmod = _w((lambda *s: np.random.randn(*s).astype(np.float32) * 0.05)(128, 6 * 128) * 128 ** (-0.5))
    _d = {'L0_attn_x': _L0_attn_in['x'], 'L0_attn_Wq': _L0_attn_in['Wq'], 'L0_attn_Wk': _L0_attn_in['Wk'], 'L0_attn_Wv': _L0_attn_in['Wv'], 'L0_attn_Wo': _L0_attn_in['Wo'], 'L0_ffn_W_r': _L0_ffn_in['W_r'], 'L0_ffn_W_k': _L0_ffn_in['W_k'], 'L0_ffn_W_v': _L0_ffn_in['W_v'], 'L0_ffn_mu_r': _L0_ffn_in['mu_r'], 'L0_ffn_mu_k': _L0_ffn_in['mu_k'], 'L0_c': _L0_c, 'L0_wmod': _L0_wmod}
    _x0 = _d['L0_attn_x']
    _d['L0_attn_x'] = jax.random.normal(jax.random.fold_in(jax.random.key(seed), 1), (8, 512, 128), dtype=_x0.dtype)
    del _x0
    return _d

def reference(L0_attn_x, L0_attn_Wq, L0_attn_Wk, L0_attn_Wv, L0_attn_Wo, L0_ffn_W_r, L0_ffn_W_k, L0_ffn_W_v, L0_ffn_mu_r, L0_ffn_mu_k, L0_c, L0_wmod):

    def _L0_attn_ref(x, Wq, Wk, Wv, Wo):
        import jax, jax.numpy as jnp
        import numpy as np
        NUM_HEADS = 16
        B, N, C = x.shape
        H = NUM_HEADS
        hd = C // H

        def proj(W):
            return (x @ W).reshape(B, N, H, 2 * hd).transpose(0, 2, 1, 3)
        q = proj(Wq)
        k = proj(Wk)
        v = proj(Wv)
        q_r, q_i = (q[..., :hd], q[..., hd:])
        k_r, k_i = (k[..., :hd], k[..., hd:])
        v_r, v_i = (v[..., :hd], v[..., hd:])
        scores = (jnp.einsum('bhnd,bhmd->bhnm', q_r, k_r) + jnp.einsum('bhnd,bhmd->bhnm', q_i, k_i)) / jnp.sqrt(jnp.float32(hd))
        causal = jnp.tril(jnp.ones((N, N), dtype=bool))
        scores = jnp.where(causal[None, None], scores, -jnp.inf)
        probs = jax.nn.softmax(scores, axis=-1)
        out_r = jnp.einsum('bhnm,bhmd->bhnd', probs, v_r)
        out_i = jnp.einsum('bhnm,bhmd->bhnd', probs, v_i)
        out = jnp.concatenate([out_r, out_i], axis=-1)
        out = out.transpose(0, 2, 1, 3).reshape(B, N, 2 * C)
        return out @ Wo

    def _L0_ffn_ref(x, W_r, W_k, W_v, mu_r, mu_k):
        import jax, jax.numpy as jnp
        import numpy as np
        DIM = 128

        def _reference_tuple_inner(x, W_r, W_k, W_v, mu_r, mu_k):
            B, T, C = x.shape
            x_prev = jnp.concatenate([jnp.zeros((B, 1, C), x.dtype), x[:, :-1, :]], axis=1)
            xr = mu_r * x + (1.0 - mu_r) * x_prev
            xk = mu_k * x + (1.0 - mu_k) * x_prev
            r = jax.nn.sigmoid(jnp.einsum('btc,dc->btd', xr, W_r))
            k = jnp.einsum('btc,dc->btd', xk, W_k)
            k_act = jnp.square(jax.nn.relu(k))
            out = r * jnp.einsum('btc,dc->btd', k_act, W_v)
            new_state = x[:, -1, :]
            return (out, new_state)
        return _reference_tuple_inner(x, W_r, W_k, W_v, mu_r, mu_k)[0]
    x = L0_attn_x
    mod = (_silu(L0_c) @ L0_wmod).reshape(L0_c.shape[0], 6, 1, -1)
    sa, ca, ga, sb, cb, gb = (mod[:, 0], mod[:, 1], mod[:, 2], mod[:, 3], mod[:, 4], mod[:, 5])
    ga = (2 * (ga >= 0) - 1) * jnp.maximum(jnp.abs(ga), 0.25)
    gb = (2 * (gb >= 0) - 1) * jnp.maximum(jnp.abs(gb), 0.25)
    h = _layernorm(x, axis=-1) * (1 + ca) + sa
    x = x + ga * _L0_attn_ref(h, L0_attn_Wq, L0_attn_Wk, L0_attn_Wv, L0_attn_Wo)
    h = _layernorm(x, axis=-1) * (1 + cb) + sb
    x = x + gb * _L0_ffn_ref(h, L0_ffn_W_r, L0_ffn_W_k, L0_ffn_W_v, L0_ffn_mu_r, L0_ffn_mu_k)
    return x

_drawn_inputs = setup_inputs


def setup_inputs(seed=0):
    import zlib

    import numpy as np

    out = dict(_drawn_inputs(seed))
    spreads = {}
    factors = {'L0_ffn_W_r': 8.0,
     'L0_ffn_W_k': 2.976,
     'L0_ffn_W_v': 2.745,
     'L0_ffn_mu_r': 8.0,
     'L0_ffn_mu_k': 4.641}
    for name, (base, spread) in spreads.items():
        noise = np.random.default_rng([zlib.crc32(name.encode()), seed]).standard_normal(out[name].shape)
        drawn = base * np.exp(spread * noise) if base else spread * noise
        out[name] = jnp.asarray(drawn.astype(out[name].dtype))
    for name, factor in factors.items():
        out[name] = (out[name] * factor).astype(out[name].dtype)
    return out
```

```python
from contextlib import ExitStack

import concourse.bass as bass
from concourse import mybir

F32 = mybir.dt.float32
BF16 = mybir.dt.bfloat16
ALU = mybir.AluOpType
ACT = mybir.ActivationFunctionType
AX_X = mybir.AxisListType.X

P = 128
HEADS = 16
HD = 16
GH = 4
STEPS = HEADS // GH
SLOTS = 12
UNITS = SLOTS * STEPS
ST, SQ = 2, 3
PARTS = 3
Q_PARTS = (0, 0, 1, 1, 0, 2)
K_PARTS = (0, 1, 0, 1, 2, 0)
STACK = HD * len(Q_PARTS)
SHIFTED = STACK + PARTS
VW = 32
MASKED = -1.0e30
LOWEST = -3.0e38
SCALE = float((HD // 2) ** -0.5)
EPS = 1e-5

SPARE = {
    "OT0": (0, 1, -1), "H2T": (0, 3, -2), "MT0": (0, 5, -1), "HT": (0, 7, 1), "KT": (0, 10, -2),
    "OT1": (1, 1, -1), "Q0": (1, 2, 1), "K0": (1, 4, 1), "MT1": (1, 5, 0), "R": (1, 8, -2),
    "V0": (1, 9, 0), "KV": (1, 10, -2),
    "OT2": (2, 1, -1), "Q1": (2, 2, 1), "K1": (2, 4, 1), "MT2": (2, 5, 0),
    "OT3": (3, 1, -1), "OB0": (3, 3, -1), "OB1": (3, 4, -1), "MT3": (3, 5, 0), "WO": (3, 7, -1),
    "V1": (3, 10, 0),
}
ORDER = list(SPARE)
GATE_SLOTS = ((0, 6), (1, 0), (1, 6), (2, 0))
P1_BLOCKS = (((3, 0),), ((2, 0),), ((0, 0), (1, P)))
LOOP_FIRST, LAG = 2, 2


def build(nc, x, Wq, Wk, Wv, Wo, W_r, W_k, W_v, mu_r, mu_k, cond, wmod, out):
    B, N, C = x.shape
    TT = N // P
    assert C == P and TT == 4 and Wq.shape[1] == HEADS * HD
    LOOP_END = B - 2
    FIRST, LAST = -1, B + 1
    KB = [0]
    for kb in range(TT):
        KB.append(KB[-1] + N - kb * P)
    PROB = KB[TT]

    with ExitStack() as ctx:
        def sb(name, shape, dt=F32):
            return ctx.enter_context(nc.sbuf_tensor(name, shape, dt))

        def sem(name):
            return ctx.enter_context(nc.semaphore(name))

        q_stack = sb("q_stack", [P, STEPS, GH, N], BF16)
        k_stack = sb("k_stack", [P, STEPS, GH, N], BF16)
        probs = sb("probs", [P, 2, GH, PROB])
        v_ones = sb("v_ones", [P, TT, HEADS, VW])
        parts = sb("parts", [P, 2, 2, PARTS, N], BF16)
        rest = sb("rest", [P, 2, N])
        x_in = sb("x_in", [P, TT, C])
        x_res = sb("x_res", [P, TT, C])
        x_norm = sb("x_norm", [P, TT, C])
        hT = sb("hT", [P, N])
        hT_v = sb("hT_v", [P, N])
        out_t = sb("out_t", [P, N])
        o_tok = sb("o_tok", [P, TT, HEADS * HD])
        o_feat = sb("o_feat", [P, 2, N])
        x1 = sb("x1", [P, TT, C])
        x1_norm = sb("x1_norm", [P, TT, C])
        h2T = sb("h2T", [P, 1 + N])
        shift_tmp = sb("shift_tmp", [P, 2, N])
        mixed = sb("mixed", [P, 2, N])
        k_relu = sb("k_relu", [P, N])
        k_act = sb("k_act", [P, N])
        tanh_r = sb("tanh_r", [P, N])
        rkv = sb("rkv", [P, TT, C])
        y = sb("y", [P, TT, C])
        wq = sb("wq", [P, HEADS * HD])
        wk = sb("wk", [P, HEADS * HD])
        wv = sb("wv", [P, HEADS * HD])
        wo = sb("wo", [P, 2, C])
        wo_gated = sb("wo_gated", [P, 2, C])
        w_rkv = sb("w_rkv", [P, 3, C])
        w_rkvT = sb("w_rkvT", [P, 3, C])
        wvT_gated = sb("wvT_gated", [P, C])
        wm = sb("wm", [P, 6 * C])
        condT = sb("condT", [P, B])
        tanh_c = sb("tanh_c", [P, B])
        silu_c = sb("silu_c", [P, B])
        silu_b = sb("silu_b", [P, B, P])
        mod_T = sb("mod_T", [P, 4, B])
        gates = sb("gates", [P, B, 2, C])
        gate_sign = sb("gate_sign", [P, 2, 2 * C])
        gate_size = sb("gate_size", [P, 2, 2 * C])
        mu = sb("mu", [P, 2])
        mu_not = sb("mu_not", [P, 2])
        ident_f = sb("ident_f", [P, P])
        ident_b = sb("ident_b", [P, P], BF16)
        causal = sb("causal", [P, N])
        max_row = sb("max_row", [P, 2, GH, TT])
        max_rest = sb("max_rest", [P, GH, TT])
        max_rest2 = sb("max_rest2", [P, GH, TT])
        shift = sb("shift", [P, 2, PARTS, GH * TT], BF16)
        shift_T = sb("shift_T", [PARTS * GH * TT, 2, P], BF16)
        stats = sb("stats", [P, 2, TT, 6])
        mean_var = sb("mean_var", [P, 2, TT, 2])
        var_eps = sb("var_eps", [P, 2, TT])
        minus_half = sb("minus_half", [P, TT])
        rstd = sb("rstd", [P, 2, TT])
        denom_inv = sb("denom_inv", [P, TT, GH])

        st_bank = [ctx.enter_context(nc.psum_tensor(f"st{i}", [P, N], F32)) for i in range(ST)]
        sq_bank = [ctx.enter_context(nc.psum_tensor(f"sq{i}", [P, N], F32)) for i in range(SQ)]
        po_bank = ctx.enter_context(nc.psum_tensor("po", [P, N], F32))
        spare = [ctx.enter_context(nc.psum_tensor(f"spare{i}", [P, N], F32)) for i in range(2)]

        scratch = nc.dram_tensor("parts_dram", [2, 2, PARTS, P, N], BF16).ap()

        st_ready = sem("st_ready")
        exp_done = sem("exp_done")
        sq_ready = sem("sq_ready")
        max_done = sem("max_done")
        dve_own = sem("dve_own")
        mixture_half = sem("mixture_half")
        stats_done = sem("stats_done")
        pool_own = sem("pool_own")
        exps_seen = sem("exps_seen")
        maxes_seen = sem("maxes_seen")
        shift_ready = sem("shift_ready")
        shift_loaded = [sem(f"shift_loaded{g}") for g in range(STEPS)]
        masked = sem("masked")
        po_ready = sem("po_ready")
        out_t_ready = sem("out_t_ready")
        ready = {u: sem(f"{u}_ready") for u in ORDER}
        read = {u: sem(f"{u}_read") for u in ORDER}
        hi_done = {u: sem(f"{u}_hi") for u in ("Q0", "K0", "Q1", "K1")}
        mid_done = {u: sem(f"{u}_mid") for u in ("Q0", "K0", "Q1", "K1")}
        lo_done = {u: sem(f"{u}_lo") for u in ("Q0", "K0", "Q1", "K1")}
        saved = [sem(f"saved{h}") for h in range(2)]
        stacked = [sem(f"stacked{g}") for g in range(STEPS)]
        x_loaded = sem("x_loaded")
        xres_loaded = sem("xres_loaded")
        norm_done = sem("norm_done")
        var_done = [sem(f"var_done{i}") for i in range(2)]
        rstd_done = [sem(f"rstd_done{i}") for i in range(2)]
        hTv_done = sem("hTv_done")
        o_tok_done = sem("o_tok_done")
        x1_norm_done = sem("x1_norm_done")
        mixed_done = sem("mixed_done")
        relu_done = sem("relu_done")
        k_act_done = sem("k_act_done")
        wo_gated_done = sem("wo_gated_done")
        wv_gated_done = sem("wv_gated_done")
        y_done = sem("y_done")
        stored = sem("stored")
        passed = {e.engine: sem(f"passed_{n}") for n, e in
                  (("pe", nc.tensor), ("dve", nc.vector), ("pool", nc.gpsimd), ("sp", nc.sync))}
        s_cond = sem("s_cond")
        s_w = sem("s_w")
        s_w2 = sem("s_w2")
        s_mu = sem("s_mu")
        s_const = sem("s_const")
        s_tanh = sem("s_tanh")
        s_silu = sem("s_silu")
        s_silub = sem("s_silub")
        s_setup_pe = sem("s_setup_pe")
        s_wT = sem("s_wT")
        s_mod = sem("s_mod")
        s_gate_units = sem("s_gate_units")
        s_gates = sem("s_gates")
        s_zero = sem("s_zero")
        s_ones = sem("s_ones")

        LOADS_W2 = 7

        def works(b):
            return 0 <= b < B

        def taken(t):
            return min(max(t - LAG, 0), LOOP_END - LOOP_FIRST)

        def left(t, db, n):
            return UNITS * (t + db - taken(t)) + n

        def group_at(g, lag):
            return (g - lag) // STEPS, (g - lag) % STEPS

        def spare_at(g, slot, t):
            return [u for u in ORDER if SPARE[u][:2] == (g, slot) and works(t + SPARE[u][2])]

        def bank_of(u):
            return spare[ORDER.index(u) % 2]

        def user_before(u, t):
            i, dt = ORDER.index(u), 0
            while t + dt >= FIRST:
                i -= 2
                if i < 0:
                    i, dt = i + len(ORDER), dt - 1
                v = ORDER[i]
                if works(t + dt + SPARE[v][2]):
                    return v, dt + SPARE[v][2]
            return None

        def apart(eng):
            eng.sem_inc(passed[eng.engine], 1)

        def iterations(eng, body):
            for t in range(FIRST, LOOP_FIRST):
                body(t, t)
            with eng.Fori(LOOP_FIRST, LOOP_END) as tv:
                body(LOOP_FIRST, tv)
            for t in range(LOOP_END, LAST + 1):
                body(t, t)

        block = ctx.enter_context(nc.Block())

        @block.sync
        def _(sp):
            sp.dma_start(condT[:, :], cond.rearrange("b c -> c b"), allow_slow_non_contiguous=True).then_inc(s_cond, 16)
            sp.dma_start(x_in[:, :, :], x[0].rearrange("(t p) c -> p t c", p=P)).then_inc(x_loaded, 16)
            sp.dma_start(wm[:, :], wmod).then_inc(s_w, 16)
            for dst, src in ((wq[:, :], Wq), (wk[:, :], Wk), (wv[:, :], Wv),
                             (wo[:, :, :], Wo.rearrange("(a p) c -> p a c", p=P)),
                             (w_rkv[:, 0, :], W_r), (w_rkv[:, 1, :], W_k), (w_rkv[:, 2, :], W_v)):
                sp.dma_start(dst, src).then_inc(s_w2, 16)
            sp.dma_start(mu[:, 0:1], mu_r.rearrange("(c o) -> c o", o=1)).then_inc(s_mu, 16)
            sp.dma_start(mu[:, 1:2], mu_k.rearrange("(c o) -> c o", o=1)).then_inc(s_mu, 16)

            def stack_group(t, tv, db, g):
                half, row = g // 2, (g % 2) * GH * HD
                sp.wait_ge(saved[half], 32 * (tv + db + 1))
                apart(sp)
                if works(t + db - 1):
                    sp.wait_ge(exps_seen, STEPS * (tv + db - 1) + g + 1)
                for i, (stack, which) in enumerate(((q_stack, Q_PARTS), (k_stack, K_PARTS))):
                    for s, part in enumerate(which):
                        sp.dma_start(
                            stack[s * HD:(s + 1) * HD, g, :, :],
                            scratch[i, half, part, row:row + GH * HD, :].rearrange("(h d) n -> d h n", d=HD),
                        ).then_inc(stacked[g], 16)

            def load_shifts(t, tv, g):
                db, pg = group_at(g, 1)
                if not works(t + db):
                    return
                sp.wait_ge(read[f"MT{g}"], tv + db + 1)
                n = GH * TT
                for i in range(PARTS):
                    sp.dma_start(q_stack[STACK + i:STACK + i + 1, pg, :, :].rearrange("o h (q n) -> o (h q) n", n=P),
                                 shift_T[i * n:(i + 1) * n, pg % 2, :]).then_inc(shift_loaded[pg], 16)

            def save_half(t, tv, half):
                if works(t):
                    for g in (2 * half, 2 * half + 1):
                        sp.wait_ge(stacked[g], 16 * 12 * (tv + 1))
                for i, u in enumerate((f"Q{half}", f"K{half}")):
                    sp.wait_ge(lo_done[u], tv + 2)
                    sp.dma_start(scratch[i, half].rearrange("a p n -> p a n"),
                                 parts[:, i, half, :, :]).then_inc(saved[half], 16)

            def body(t, tv):
                for g in range(STEPS):
                    if g < STEPS - 1 and works(t):
                        stack_group(t, tv, 0, g + 1)
                    if g == STEPS - 1 and works(t + 1):
                        if t > FIRST:
                            stack_group(t, tv, 1, 0)
                    load_shifts(t, tv, g)
                    if g == 0 and works(t - 1):
                        if works(t - 2):
                            sp.wait_ge(read["WO"], tv - 1)
                            apart(sp)
                        sp.dma_start(x_res[:, :, :], x[tv - 1].rearrange("(t p) c -> p t c", p=P)
                                     ).then_inc(xres_loaded, 16)
                    if g == 1 and works(t + 2):
                        sp.wait_ge(norm_done, tv + 2)
                        apart(sp)
                        sp.dma_start(x_in[:, :, :], x[tv + 2].rearrange("(t p) c -> p t c", p=P)
                                     ).then_inc(x_loaded, 16)
                    if g == 1 and works(t + 1):
                        save_half(t, tv, 0)
                        if t == FIRST:
                            stack_group(t, tv, 1, 0)
                    if g == 2 and works(t - 2):
                        sp.wait_ge(y_done, tv - 1)
                        apart(sp)
                        sp.dma_start(out[tv - 2].rearrange("(t p) c -> p t c", p=P), y[:, :, :]
                                     ).then_inc(stored, 16)
                    if g == 2 and works(t + 1):
                        save_half(t, tv, 1)

            iterations(sp, body)
            sp.wait_ge(stored, 16 * B)
            for h in range(2):
                sp.wait_ge(saved[h], 32 * B)

        @block.tensor
        def _(pe):
            pe.wait_ge(s_w, 16)
            pe.wait_ge(s_silu, 1)
            for i, j in enumerate((0, 1, 3, 4)):
                last = nc.tensor.matmul(st_bank[1][:, i * B:(i + 1) * B], lhsT=wm[:, j * C:(j + 1) * C],
                                        rhs=silu_c[:, :], start=True, stop=True)
            last.then_inc(s_setup_pe, 1)
            pe.wait_ge(s_const, 1)

            def setup_rest():
                pe.wait_ge(s_w2, 16 * LOADS_W2)
                for i in range(3):
                    last = nc.tensor.transpose(st_bank[0][:, i * C:(i + 1) * C], w_rkv[:, i, :], ident_f[:, :])
                last.then_inc(s_setup_pe, 1)
                pe.wait_ge(s_wT, 1)
                pe.wait_ge(s_mod, 4)

            def gate_unit(n):
                pe.wait_ge(s_silub, 1)
                if n:
                    pe.wait_ge(s_gates, n)
                for b in (2 * n, 2 * n + 1):
                    for i, j in enumerate((2, 5)):
                        at = (b % 2) * 2 * C + i * C
                        last = nc.tensor.matmul(po_bank[:, at:at + C], lhsT=silu_b[:, b, :],
                                                rhs=wm[:, j * C:(j + 1) * C], start=True, stop=True)
                last.then_inc(s_gate_units, 1)

            def p2_unit(t, tv, g, slot):
                db, pg = group_at(g, 2)
                if not works(t + db):
                    return
                h, j = divmod(slot, 3)
                if slot == 0:
                    pe.wait_ge(shift_loaded[pg], 48 * (tv + db + 1))
                unit = SLOTS * pg + slot
                if UNITS * (t + db) + unit >= ST:
                    pe.wait_ge(exp_done, left(t, db, unit - ST + 1))
                ps = st_bank[slot % ST]
                for kb, at in (((0, 0),), ((1, 0),), ((2, 0), (3, 2 * P)))[j]:
                    last = nc.tensor.matmul(ps[:, at:at + N - kb * P],
                                            lhsT=k_stack[0:SHIFTED, pg, h, kb * P:(kb + 1) * P],
                                            rhs=q_stack[0:SHIFTED, pg, h, kb * P:N], start=True, stop=True)
                last.then_inc(st_ready, 1)

            def p1_unit(t, tv, g, slot):
                if not works(t):
                    return
                h, j = divmod(slot, 3)
                if slot == 0:
                    pe.wait_ge(stacked[g], 16 * 12 * (tv + 1))
                unit = SLOTS * g + slot
                if UNITS * t + unit >= SQ:
                    pe.wait_ge(max_done, left(t, 0, unit - SQ + 1))
                ps = sq_bank[slot % SQ]
                for qb, at in P1_BLOCKS[j]:
                    end = at + (qb + 1) * P
                    last = nc.tensor.matmul(ps[:, at:end], lhsT=q_stack[0:STACK, g, h, qb * P:(qb + 1) * P],
                                            rhs=k_stack[0:STACK, g, h, 0:(qb + 1) * P], start=True, stop=True)
                last.then_inc(sq_ready, 1)

            def pv_block(t, tv, g, kb):
                db, pg = group_at(g, 3)
                if not works(t + db):
                    return
                if kb == 0:
                    if STEPS * (t + db) + pg > 0:
                        pe.wait_ge(out_t_ready, STEPS * (tv + db) + pg)
                    else:
                        pe.wait_ge(s_gates, B // 2)
                    pe.wait_ge(read["V1" if pg >= 2 else "V0"], tv + db + 1)
                pe.wait_ge(masked, TT * (STEPS * (tv + db) + pg) + kb + 1)
                for h in range(GH):
                    last = nc.tensor.matmul(po_bank[h * VW:(h + 1) * VW, kb * P:N],
                                            lhsT=v_ones[:, kb, pg * GH + h, :],
                                            rhs=probs[:, pg % 2, h, KB[kb]:KB[kb + 1]],
                                            start=kb == 0, stop=kb == TT - 1)
                if kb == TT - 1:
                    last.then_inc(po_ready, 1)

            def spare_unit(u, t, tv):
                g, _, db = SPARE[u]
                b1 = tv + db + 1
                before = user_before(u, t)
                if before:
                    pe.wait_ge(read[before[0]], tv + before[1] + 1)
                ps = bank_of(u)
                if u.startswith("OT"):
                    pe.wait_ge(out_t_ready, STEPS * (tv + db) + g + 1)
                    for i in range(TT):
                        last = nc.tensor.transpose(ps[:, i * P:(i + 1) * P], out_t[:, i * P:(i + 1) * P],
                                                   ident_f[:, :])
                elif u in ("HT", "H2T"):
                    pe.wait_ge(norm_done if u == "HT" else x1_norm_done, b1)
                    src = x_norm if u == "HT" else x1_norm
                    for i in range(TT):
                        last = nc.tensor.transpose(ps[:, i * P:(i + 1) * P], src[:, i, :], ident_f[:, :])
                elif u.startswith("MT"):
                    _, pg = group_at(g, 1)
                    pe.wait_ge(shift_ready, STEPS * (tv + db) + pg + 1)
                    apart(pe)
                    last = nc.tensor.transpose(ps[0:PARTS * GH * TT, 0:P // 2].bitcast(BF16),
                                               shift[:, pg % 2, :, :], ident_b[:, :])
                elif u[0] in "QK" and u[1] in "01":
                    half = int(u[1])
                    if t == FIRST:
                        pe.wait_ge(s_w2, 16 * LOADS_W2)
                    pe.wait_ge(read["HT"], b1)
                    w = wq if u[0] == "Q" else wk
                    last = nc.tensor.matmul(ps[:, :], lhsT=w[:, half * P:(half + 1) * P], rhs=hT[:, :],
                                            start=True, stop=True)
                elif u in ("V0", "V1"):
                    half = int(u[1])
                    pe.wait_ge(hTv_done, b1)
                    for i in range(TT):
                        last = nc.tensor.matmul(ps[:, i * P:(i + 1) * P], lhsT=hT_v[:, i * P:(i + 1) * P],
                                                rhs=wv[:, half * P:(half + 1) * P], start=True, stop=True)
                elif u in ("OB0", "OB1"):
                    half = int(u[2])
                    pe.wait_ge(o_tok_done, STEPS * b1 if half else STEPS * (tv + db) + 2)
                    for i in range(TT):
                        last = nc.tensor.transpose(ps[:, i * P:(i + 1) * P],
                                                   o_tok[:, i, half * P:(half + 1) * P], ident_f[:, :])
                elif u == "WO":
                    pe.wait_ge(read["OB1"], b1)
                    pe.wait_ge(wo_gated_done, b1)
                    for i in range(TT):
                        for a in range(2):
                            last = nc.tensor.matmul(ps[:, i * P:(i + 1) * P],
                                                    lhsT=o_feat[:, a, i * P:(i + 1) * P],
                                                    rhs=wo_gated[:, a, :], start=a == 0, stop=a == 1)
                elif u == "KT":
                    pe.wait_ge(mixed_done, 2 * (tv + db) + 1)
                    last = nc.tensor.matmul(ps[:, :], lhsT=w_rkvT[:, 1, :], rhs=mixed[:, 1, :],
                                            start=True, stop=True)
                elif u == "R":
                    pe.wait_ge(mixed_done, 2 * b1)
                    for i in range(TT):
                        last = nc.tensor.matmul(ps[:, i * P:(i + 1) * P], lhsT=mixed[:, 0, i * P:(i + 1) * P],
                                                rhs=w_rkvT[:, 0, :], start=True, stop=True)
                elif u == "KV":
                    pe.wait_ge(k_act_done, b1)
                    pe.wait_ge(wv_gated_done, b1)
                    for i in range(TT):
                        last = nc.tensor.matmul(ps[:, i * P:(i + 1) * P], lhsT=k_act[:, i * P:(i + 1) * P],
                                                rhs=wvT_gated[:, :], start=True, stop=True)
                last.then_inc(ready[u], 1)

            def body(t, tv):
                for g in range(STEPS):
                    if t == FIRST and g == 3:
                        setup_rest()
                    for slot in range(SLOTS):
                        p2_unit(t, tv, g, slot)
                        p1_unit(t, tv, g, slot)
                        if slot == ST - 1:
                            db, pg = group_at(g, 3)
                            if works(t + db):
                                if (works(t + group_at(g, 2)[0])) is False:
                                    pe.wait_ge(exp_done, left(t, db, SLOTS * (pg + 1)))
                                pe.sem_inc(exps_seen, 1)
                        if slot == SQ - 1:
                            db, pg = group_at(g, 1)
                            if works(t + db):
                                if not works(t):
                                    pe.wait_ge(max_done, left(t, db, SLOTS * (pg + 1)))
                                pe.sem_inc(maxes_seen, 1)
                        if t == 0 and (g, slot) in GATE_SLOTS:
                            gate_unit(GATE_SLOTS.index((g, slot)))
                        for u in spare_at(g, slot, t):
                            spare_unit(u, t, tv)
                        if slot >= SLOTS - 1 - TT and slot < SLOTS - 1:
                            pv_block(t, tv, g, slot - (SLOTS - 1 - TT))
                if t == LOOP_FIRST:
                    pe.sem_inc(exp_done, -UNITS)
                    pe.sem_inc(max_done, -UNITS)

            iterations(pe, body)

        @block.scalar
        def _(act):
            act.wait_ge(s_cond, 16)
            nc.scalar.activation(tanh_c[:, :], condT[:, :], ACT.Tanh, scale=0.5).then_inc(s_tanh, 1)

            def exp_unit(t, tv, g, slot):
                db, pg = group_at(g, 2)
                if not works(t + db):
                    return
                h, j = divmod(slot, 3)
                if slot == 0 and STEPS * (t + db) + pg >= 2:
                    act.wait_ge(po_ready, STEPS * (tv + db) + pg - 1)
                act.wait_ge(st_ready, left(t, db, SLOTS * pg + slot + 1))
                lo, hi = (KB[0], KB[1], KB[2], KB[4])[j:j + 2]
                nc.scalar.activation(probs[:, pg % 2, h, lo:hi], st_bank[slot % ST][:, 0:hi - lo], ACT.Exp,
                                     scale=SCALE).then_inc(exp_done, 1)

            def copy_out(t, tv, g):
                db, pg = group_at(g, 3)
                if not works(t + db):
                    return
                if STEPS * (t + db) + pg > 0:
                    act.wait_ge(ready[f"OT{(pg - 1) % STEPS}"], tv + db + (1 if pg else 0))
                act.wait_ge(po_ready, STEPS * (tv + db) + pg + 1)
                nc.scalar.copy(out_t[:, :], po_bank[:, :]).then_inc(out_t_ready, 1)

            def spare_read(u, t, tv):
                g, _, db = SPARE[u]
                b1 = tv + db + 1
                ps = bank_of(u)
                if u in ("H2T", "HT"):
                    act.wait_ge(ready[u], b1)
                    dst, i = (hT[:, :], 0) if u == "HT" else (h2T[:, 1:1 + N], 2)
                    if u == "HT":
                        act.wait_ge(s_mod, 4)
                        if works(t):
                            act.wait_ge(hTv_done, tv + 1)
                    elif works(t - 3):
                        act.wait_ge(mixed_done, 2 * (tv - 2))
                    b = bass.ds(tv + db, 1)
                    nc.scalar.activation(dst, ps[:, :], ACT.Identity, bias=mod_T[:, i, b],
                                         scale=mod_T[:, i + 1, b]).then_inc(read[u], 1)
                elif u.startswith("MT"):
                    act.wait_ge(ready[u], b1)
                    _, pg = group_at(g, 1)
                    if STEPS * (t + db) + pg >= 2:
                        sg, sdb = (pg - 2) % STEPS, db + (pg - 2) // STEPS
                        act.wait_ge(shift_loaded[sg], 48 * (tv + sdb + 1))
                    nc.scalar.copy(shift_T[:, pg % 2, :], ps[0:PARTS * GH * TT, 0:P // 2].bitcast(BF16)
                                   ).then_inc(read[u], 1)
                elif u == "KT":
                    act.wait_ge(ready[u], b1)
                    if works(t - 3):
                        act.wait_ge(k_act_done, tv - 2)
                    nc.scalar.activation(k_relu[:, :], ps[:, :], ACT.Relu).then_inc(read[u], 1)
                elif u[0] in "QK" and u[1] in "01":
                    half = int(u[1])
                    act.wait_ge(ready[u], b1)
                    if works(t):
                        act.wait_ge(saved[half], 32 * (tv + 1))
                    nc.scalar.copy(parts[:, 0 if u[0] == "Q" else 1, half, 0, :], ps[:, :]
                                   ).then_inc(hi_done[u], 1)
                elif u == "R":
                    act.wait_ge(ready[u], b1)
                    if works(t - 3):
                        act.wait_ge(read["KV"], tv - 2)
                    nc.scalar.activation(tanh_r[:, :], ps[:, :], ACT.Tanh, scale=0.5).then_inc(read[u], 1)
                elif u in ("V0", "V1"):
                    half = int(u[1])
                    act.wait_ge(ready[u], b1)
                    if t == 0 and half == 0:
                        act.wait_ge(s_ones, 1)
                    hh = HEADS // 2
                    dst = v_ones[:, :, half * hh:(half + 1) * hh, 0:HD]
                    nc.scalar.copy(dst, ps[:, :].rearrange("p (t h d) -> p t h d", t=TT, d=HD)
                                   ).then_inc(read[u], 1)
                elif u in ("OB0", "OB1"):
                    half = int(u[2])
                    act.wait_ge(ready[u], b1)
                    if works(t - 2):
                        act.wait_ge(ready["WO"], tv - 1)
                    nc.scalar.copy(o_feat[:, half, :], ps[:, :]).then_inc(read[u], 1)

            def body(t, tv):
                for g in range(STEPS):
                    for slot in range(SLOTS + 1):
                        if slot < SLOTS:
                            exp_unit(t, tv, g, slot)
                        if slot > 0:
                            for u in spare_at(g, slot - 1, t):
                                spare_read(u, t, tv)
                    copy_out(t, tv, g)
                if t == LOOP_FIRST:
                    act.sem_inc(st_ready, -UNITS)

            iterations(act, body)

        @block.vector
        def _(dve):
            def own(ins):
                ins.then_inc(dve_own, 1)
                dve.wait_ge(dve_own, 1)
                dve.sem_inc(dve_own, -1)

            def norm_stats(src, i, first):
                for a in (first, first + 1):
                    last = nc.vector.bn_stats(stats[:, i, a, :], src[:, a, :])
                if first:
                    last.then_inc(stats_done, 1)

            def norm_aggr(i):
                dve.wait_ge(stats_done, 1)
                dve.sem_inc(stats_done, -1)
                for a in range(TT):
                    last = nc.vector.bn_aggr(mean_var[:, i, a, :], stats[:, i, a, :])
                last.then_inc(var_done[i], 1)

            nc.vector.memset(h2T[:, 0:1], 0.0).then_inc(s_zero, 1)
            dve.wait_ge(x_loaded, 16)
            norm_stats(x_in, 0, 0)
            norm_stats(x_in, 0, 2)
            norm_aggr(0)
            dve.wait_ge(s_tanh, 1)
            own(nc.vector.scalar_tensor_tensor(out=tanh_c[:, :], in0=tanh_c[:, :], scalar=1.0,
                                               in1=condT[:, :], op0=ALU.add, op1=ALU.mult))
            nc.vector.tensor_scalar(silu_c[:, :], tanh_c[:, :], 0.5, None, ALU.mult).then_inc(s_silu, 1)
            dve.wait_ge(s_setup_pe, 1)
            for i in range(4):
                nc.vector.tensor_scalar(mod_T[:, i, :], st_bank[1][:, i * B:(i + 1) * B], float(i % 2), None,
                                        ALU.add).then_inc(s_mod, 1)

            def setup_rest():
                nc.vector.tensor_scalar(silu_b[:, :, :], tanh_c[:, :].unsqueeze(2).to_broadcast([P, B, P]),
                                        0.5, None, ALU.mult).then_inc(s_silub, 1)
                dve.wait_ge(s_mu, 32)
                nc.vector.tensor_scalar(mu_not[:, :], mu[:, :], -1.0, 1.0, ALU.mult, ALU.add
                                        ).then_inc(s_zero, 1)
                dve.wait_ge(s_setup_pe, 2)
                nc.vector.tensor_copy(w_rkvT[:, :, :], st_bank[0][:, 0:3 * C].rearrange("p (a c) -> p a c", a=3)
                                      ).then_inc(s_wT, 1)

            def gate_read(n):
                dve.wait_ge(s_gate_units, n + 1)
                pair = po_bank[:, :].rearrange("p (b c) -> p b c", b=2)
                own(nc.vector.tensor_scalar(gate_sign[:, :, :], pair, 0.25, None, ALU.max))
                own(nc.vector.scalar_tensor_tensor(out=gate_size[:, :, :], in0=pair, scalar=-1.0,
                                                   in1=gate_sign[:, :, :], op0=ALU.mult, op1=ALU.max))
                own(nc.vector.tensor_scalar(gate_sign[:, :, :], pair, 0.0, 2.0, ALU.is_ge, ALU.mult))
                own(nc.vector.scalar_tensor_tensor(
                    out=gates[:, 2 * n:2 * n + 2, :, :].rearrange("p b a c -> p b (a c)"),
                    in0=gate_sign[:, :, :], scalar=-1.0, in1=gate_size[:, :, :],
                    op0=ALU.add, op1=ALU.mult))
                nc.vector.tensor_scalar(gates[:, 2 * n:2 * n + 2, 1, :], gates[:, 2 * n:2 * n + 2, 1, :],
                                        0.5, None, ALU.mult).then_inc(s_gates, 1)

            def max_unit(t, tv, g, slot):
                h, j = divmod(slot, 3)
                if slot == 0 and STEPS * t + g >= 2:
                    gg = STEPS * t + g - 1
                    dve.wait_ge(shift_ready, STEPS * tv + g - 1)
                    apart(dve)
                dve.wait_ge(sq_ready, left(t, 0, SLOTS * g + slot + 1))
                ps = sq_bank[slot % SQ]
                for qb, at in P1_BLOCKS[j]:
                    row = ps[:, at:at + (qb + 1) * P]
                    last = nc.vector.tensor_tensor_reduce(
                        out=row, in0=row, in1=causal[:, N - (qb + 1) * P:N], scale=1.0, scalar=LOWEST,
                        op0=ALU.add, op1=ALU.max, accum_out=max_row[:, g % 2, h, qb:qb + 1])
                last.then_inc(max_done, 1)

            def norm_apply(src, dst, i, done, b1):
                dve.wait_ge(rstd_done[i], b1)
                for a in range(TT):
                    last = nc.vector.tensor_scalar(dst[:, a, :], src[:, a, :], mean_var[:, i, a, 0:1],
                                                   rstd[:, i, a:a + 1], ALU.subtract, ALU.mult)
                last.then_inc(done, 1)

            def copy_hT(t, tv):
                dve.wait_ge(read["HT"], tv + 1)
                if works(t - 1):
                    dve.wait_ge(ready["V1"], tv)
                nc.vector.tensor_copy(hT_v[:, :], hT[:, :]).then_inc(hTv_done, 1)

            def mixture_start(t, tv, i):
                dve.wait_ge(read["H2T"], tv - 1)
                if t == LAG:
                    dve.wait_ge(s_zero, 2)
                nc.vector.tensor_scalar(shift_tmp[:, i, :], h2T[:, 0:N], mu_not[:, i:i + 1], None,
                                        ALU.mult).then_inc(mixture_half, 1)

            def mixture_end(t, tv, i):
                dve.wait_ge(mixture_half, 1)
                dve.sem_inc(mixture_half, -1)
                if works(t - 3):
                    dve.wait_ge(ready["KT" if i else "R"], tv - 2)
                nc.vector.scalar_tensor_tensor(out=mixed[:, i, :], in0=h2T[:, 1:1 + N],
                                               scalar=mu[:, i:i + 1], in1=shift_tmp[:, i, :],
                                               op0=ALU.mult, op1=ALU.add).then_inc(mixed_done, 1)

            def spare_read(u, t, tv):
                g, _, db = SPARE[u]
                b1 = tv + db + 1
                ps = bank_of(u)
                if u.startswith("OT"):
                    dve.wait_ge(ready[u], b1)
                    if g == 0 and works(t - 2):
                        dve.wait_ge(ready["OB1"], tv - 1)
                    o = ps[:, :].rearrange("p (t h w) -> p t h w", t=TT, w=VW)
                    own(nc.vector.reciprocal(denom_inv[:, :, :], o[:, :, :, HD]))
                    dst = o_tok[:, :, g * GH * HD:(g + 1) * GH * HD].rearrange("p t (h d) -> p t h d", d=HD)
                    nc.vector.tensor_tensor(dst, o[:, :, :, 0:HD],
                                            denom_inv[:, :, :].unsqueeze(3).to_broadcast([P, TT, GH, HD]),
                                            ALU.mult).then_inc(read[u], 1)
                    dve.wait_ge(read[u], b1)
                    dve.sem_inc(o_tok_done, 1)
                elif u[0] in "QK" and u[1] in "01":
                    i, half = (0 if u[0] == "Q" else 1), int(u[1])
                    dve.wait_ge(hi_done[u], b1)
                    if half:
                        dve.wait_ge(lo_done[u[0] + "0"], b1)
                    elif works(t):
                        dve.wait_ge(lo_done[u[0] + "1"], tv + 1)
                    nc.vector.tensor_tensor(rest[:, i, :], ps[:, :], parts[:, i, half, 0, :], ALU.subtract
                                            ).then_inc(read[u], 1)
                    dve.wait_ge(read[u], b1)
                    nc.vector.tensor_copy(parts[:, i, half, 1, :], rest[:, i, :]).then_inc(mid_done[u], 1)
                elif u == "WO":
                    dve.wait_ge(ready[u], b1)
                    dve.wait_ge(xres_loaded, 16 * b1)
                    if works(t - 2):
                        dve.wait_ge(y_done, tv - 1)
                    nc.vector.tensor_tensor(x1[:, :, :], ps[:, :].rearrange("p (t c) -> p t c", t=TT),
                                            x_res[:, :, :], ALU.add).then_inc(read[u], 1)
                    dve.wait_ge(read[u], b1)
                    norm_stats(x1, 1, 0)
                    norm_stats(x1, 1, 2)
                elif u == "KV":
                    dve.wait_ge(ready[u], b1)
                    dve.wait_ge(read["R"], b1)
                    if works(t - 3):
                        dve.wait_ge(y_done, tv - 2)
                    nc.vector.scalar_tensor_tensor(out=rkv[:, :, :],
                                                   in0=tanh_r[:, :].rearrange("p (t c) -> p t c", t=TT),
                                                   scalar=1.0, in1=ps[:, :].rearrange("p (t c) -> p t c", t=TT),
                                                   op0=ALU.add, op1=ALU.mult).then_inc(read[u], 1)

            def body(t, tv):
                for g in range(STEPS):
                    for slot in range(SLOTS + 1):
                        if slot < SLOTS and works(t):
                            max_unit(t, tv, g, slot)
                        if g == 0 and works(t + 1):
                            if slot == 3:
                                if works(t):
                                    dve.wait_ge(ready["HT"], tv + 1)
                                norm_apply(x_in, x_norm, 0, norm_done, tv + 2)
                        if g == 2 and works(t + 2):
                            if slot == 7:
                                dve.wait_ge(x_loaded, 16 * (tv + 3))
                                norm_stats(x_in, 0, 0)
                            elif slot == 8:
                                norm_stats(x_in, 0, 2)
                            elif slot == 10:
                                norm_aggr(0)
                        if g == 0 and slot == 6 and works(t):
                            copy_hT(t, tv)
                        if g == 0 and works(t - 2):
                            if slot == 6:
                                mixture_start(t, tv, 1)
                            elif slot == 7:
                                mixture_end(t, tv, 1)
                            elif slot == 9:
                                mixture_start(t, tv, 0)
                            elif slot == 10:
                                mixture_end(t, tv, 0)
                        if t == 0 and (g, slot - 1) in GATE_SLOTS:
                            gate_read(GATE_SLOTS.index((g, slot - 1)))
                        if slot > 0:
                            for u in spare_at(g, slot - 1, t):
                                spare_read(u, t, tv)
                        if g == STEPS - 1 and slot == 10 and works(t - 1):
                            norm_aggr(1)
                        if g == STEPS - 1 and slot == SLOTS and works(t - 1):
                            if works(t - 2):
                                dve.wait_ge(ready["H2T"], tv - 1)
                            norm_apply(x1, x1_norm, 1, x1_norm_done, tv)
                    if t == FIRST and g == 2:
                        setup_rest()
                if t == LOOP_FIRST:
                    dve.sem_inc(sq_ready, -UNITS)

            iterations(dve, body)

        @block.gpsimd
        def _(pool):
            def own(ins):
                ins.then_inc(pool_own, 1)
                pool.wait_ge(pool_own, 1)
                pool.sem_inc(pool_own, -1)

            own(nc.gpsimd.memset(minus_half[:, :], -0.5))
            own(nc.gpsimd.memset(ident_f[:, :], 0.0))
            own(nc.gpsimd.memset(ident_b[:, :], 0.0))
            own(nc.gpsimd.memset(causal[:, :], 0.0))
            nc.gpsimd.affine_select(out=causal[:, N - P:N], in_=causal[:, N - P:N], compare_op=ALU.is_ge, fill=MASKED,
                                    base=0, pattern=[[-1, P]], channel_multiplier=1)
            nc.gpsimd.affine_select(out=ident_b[:, :], in_=ident_b[:, :], compare_op=ALU.not_equal, fill=1.0,
                                    base=0, pattern=[[-1, P]], channel_multiplier=1)
            nc.gpsimd.affine_select(out=ident_f[:, :], in_=ident_f[:, :], compare_op=ALU.not_equal, fill=1.0,
                                    base=0, pattern=[[-1, P]], channel_multiplier=1).then_inc(s_const, 1)

            def shift_rows(t, tv, g):
                db, pg = group_at(g, 1)
                if not works(t + db):
                    return
                b = pg % 2
                pool.wait_ge(maxes_seen, STEPS * (tv + db) + pg + 1)
                apart(pool)
                own(nc.gpsimd.tensor_scalar(shift[:, b, 0, :].rearrange("p (h q) -> p h q", q=TT),
                                            max_row[:, b, :, :], -1.0, None, ALU.mult))
                own(nc.gpsimd.tensor_tensor(max_rest[:, :, :], max_row[:, b, :, :],
                                            shift[:, b, 0, :].rearrange("p (h q) -> p h q", q=TT), ALU.add))
                own(nc.gpsimd.tensor_scalar(shift[:, b, 1, :].rearrange("p (h q) -> p h q", q=TT),
                                            max_rest[:, :, :], -1.0, None, ALU.mult))
                own(nc.gpsimd.tensor_tensor(max_rest2[:, :, :], max_rest[:, :, :],
                                            shift[:, b, 1, :].rearrange("p (h q) -> p h q", q=TT), ALU.add))
                nc.gpsimd.tensor_scalar(shift[:, b, 2, :].rearrange("p (h q) -> p h q", q=TT),
                                        max_rest2[:, :, :], -1.0, None, ALU.mult).then_inc(shift_ready, 1)

            def mask_probs(t, tv, g):
                db, pg = group_at(g, 3)
                if not works(t + db):
                    return
                pool.wait_ge(exps_seen, STEPS * (tv + db) + pg + 1)
                apart(pool)
                for kb in range(TT):
                    d = probs[:, pg % 2, :, KB[kb]:KB[kb] + P]
                    nc.gpsimd.affine_select(out=d, in_=d, compare_op=ALU.is_ge, fill=0.0, base=0,
                                            pattern=[[0, GH], [1, P]], channel_multiplier=-1
                                            ).then_inc(masked, 1)

            def inverse_std(i, b1):
                pool.wait_ge(var_done[i], b1)
                apart(pool)
                own(nc.gpsimd.tensor_scalar(var_eps[:, i, :], mean_var[:, i, :, 1], EPS, None, ALU.add))
                nc.gpsimd.tensor_tensor(rstd[:, i, :], var_eps[:, i, :], minus_half[:, :], ALU.pow
                                        ).then_inc(rstd_done[i], 1)

            def low_part(t, tv, u):
                i, half = (0 if u[0] == "Q" else 1), int(u[1])
                pool.wait_ge(mid_done[u], tv + 2)
                nc.gpsimd.tensor_tensor(parts[:, i, half, 2, :], rest[:, i, :], parts[:, i, half, 1, :],
                                        ALU.subtract).then_inc(lo_done[u], 1)

            def body(t, tv):
                for g in range(STEPS):
                    shift_rows(t, tv, g)
                    mask_probs(t, tv, g)
                    if g == 0 and works(t - 1):
                        if t == 1:
                            pool.wait_ge(s_gates, B // 2)
                            pool.wait_ge(s_w2, 16 * LOADS_W2)
                        if works(t - 2):
                            pool.wait_ge(ready["WO"], tv - 1)
                        nc.gpsimd.tensor_tensor(wo_gated[:, :, :], wo[:, :, :],
                                                gates[:, bass.ds(tv - 1, 1), 0, :].to_broadcast([P, 2, C]),
                                                ALU.mult).then_inc(wo_gated_done, 1)
                    if g == 0 and works(t - 2):
                        if t == 2:
                            pool.wait_ge(s_wT, 1)
                        if works(t - 3):
                            pool.wait_ge(ready["KV"], tv - 2)
                        nc.gpsimd.tensor_tensor(wvT_gated[:, :], w_rkvT[:, 2, :],
                                                gates[:, bass.ds(tv - 2, 1), 1, :].squeeze(1),
                                                ALU.mult).then_inc(wv_gated_done, 1)
                        pool.wait_ge(read["KT"], tv - 1)
                        if works(t - 3):
                            pool.wait_ge(ready["KV"], tv - 2)
                        nc.gpsimd.tensor_tensor(k_act[:, :], k_relu[:, :], k_relu[:, :], ALU.mult
                                                ).then_inc(k_act_done, 1)
                    if g in (1, 2) and works(t + 1):
                        for u in (f"Q{g - 1}", f"K{g - 1}"):
                            low_part(t, tv, u)
                    if g == 1 and works(t - 2):
                        pool.wait_ge(read["KV"], tv - 1)
                        if works(t - 3):
                            pool.wait_ge(stored, 16 * (tv - 2))
                        nc.gpsimd.tensor_tensor(y[:, :, :], rkv[:, :, :], x1[:, :, :], ALU.add
                                                ).then_inc(y_done, 1)
                    if g == 2 and works(t + 2):
                        inverse_std(0, tv + 3)
                    if g == STEPS - 1 and works(t - 1):
                        inverse_std(1, tv)
                    if g == STEPS - 1 and t == FIRST:
                        pool.wait_ge(lo_done["K1"], 1)
                        pool.wait_ge(rstd_done[0], 2)
                        own(nc.gpsimd.memset(k_stack[STACK:P, :, :, :], 1.0))
                        nc.gpsimd.memset(v_ones[:, :, :, HD:VW], 1.0).then_inc(s_ones, 1)

            inverse_std(0, 1)
            iterations(pool, body)


_INS = ['L0_attn_x', 'L0_attn_Wq', 'L0_attn_Wk', 'L0_attn_Wv', 'L0_attn_Wo', 'L0_ffn_W_r', 'L0_ffn_W_k',
        'L0_ffn_W_v', 'L0_ffn_mu_r', 'L0_ffn_mu_k', 'L0_c', 'L0_wmod']


def kernel(**inputs):
    import numpy as _np
    import concourse.bacc as _bacc
    from concourse import mybir as _mybir
    from concourse.bass_utils import run_bass_kernel_spmd as _run

    nc = _bacc.Bacc("TRN2", target_bir_lowering=False, num_devices=1)
    arrays, args = {}, []
    for name in _INS:
        a = _np.ascontiguousarray(inputs[name])
        arrays[f"in_{name}_dram"] = a
        args.append(nc.dram_tensor(f"in_{name}_dram", a.shape, _mybir.dt.from_np(a.dtype), kind="ExternalInput").ap())
    shape = inputs['L0_attn_x'].shape
    args.append(nc.dram_tensor("out_0_dram", shape, _mybir.dt.float32, kind="ExternalOutput").ap())
    build(nc, *args)
    r = _run(nc, [arrays], core_ids=[0])
    return r.results[0]["out_0_dram"]
```

```python
from contextlib import ExitStack

import concourse.bass as bass
from concourse import mybir

F32 = mybir.dt.float32
BF16 = mybir.dt.bfloat16
ALU = mybir.AluOpType
ACT = mybir.ActivationFunctionType
AX_X = mybir.AxisListType.X

P = 128
HEADS = 16
HD = 16
GH = 4
STEPS = HEADS // GH
SLOTS = 12
UNITS = SLOTS * STEPS
ST, SQ = 2, 3
PARTS = 3
Q_PARTS = (0, 1, 2, 0, 1, 0)
K_PARTS = (0, 0, 0, 1, 1, 2)
BLOCK_RUNS = ((0, 3), (3, 5), (5, 6))
STACK = HD * len(Q_PARTS)
SHIFTED = STACK + PARTS
VW = 32
MASKED = -1.0e30
LOWEST = -3.0e38
SCALE = float((HD // 2) ** -0.5)
EPS = 1e-5

SPARE = {
    "V1": (0, 0, -1), "HT": (0, 3, 1), "MT0": (0, 5, -1), "H2T": (0, 6, -2),
    "KT": (1, 0, -2), "R": (1, 3, -2), "Q0": (1, 4, 1), "MT1": (1, 5, 0), "K0": (1, 10, 1),
    "KV": (2, 0, -2), "V0": (2, 3, 0), "Q1": (2, 4, 1), "MT2": (2, 5, 0), "K1": (2, 10, 1),
    "OB0": (3, 1, -1), "MT3": (3, 5, 0), "OB1": (3, 6, -1), "WO": (3, 8, -1),
}
ORDER = list(SPARE)
TURNS = {f"OT{g}": (g, 2, -1) for g in range(STEPS)}
UNIT_AT = {**TURNS, **SPARE}
PV_SLOT = 6
COPY_SLOT = 10
GATE_SLOTS = ((0, 6), (1, 0), (1, 6), (2, 0))
P1_BLOCKS = (((3, 0),), ((2, 0),), ((0, 0), (1, P)))
LOOP_FIRST, LAG = 2, 2


def build(nc, x, cond_mod, qk_weights, weights, out):
    B, N, C = x.shape
    TT = N // P
    assert C == P and TT == 4 and qk_weights.shape[1] == 2 * HEADS * HD
    LOOP_END = B - 2
    FIRST, LAST = -1, B + 1
    KB = [0]
    for kb in range(TT):
        KB.append(KB[-1] + N - kb * P)
    PROB = KB[TT]

    with ExitStack() as ctx:
        def sb(name, shape, dt=F32):
            return ctx.enter_context(nc.sbuf_tensor(name, shape, dt))

        def sem(name):
            return ctx.enter_context(nc.semaphore(name))

        q_stack = sb("q_stack", [P, STEPS, GH, N], BF16)
        k_stack = sb("k_stack", [P, STEPS, GH, N], BF16)
        probs = sb("probs", [P, 2, GH, PROB])
        v_ones = sb("v_ones", [P, TT, HEADS, VW])
        parts = sb("parts", [P, 2, 2, PARTS, N], BF16)
        rest = sb("rest", [P, 2, N])
        x_in = sb("x_in", [P, TT, C])
        x_res = sb("x_res", [P, TT, C])
        x_norm = sb("x_norm", [P, TT, C])
        hT = sb("hT", [P, N])
        hT_v = sb("hT_v", [P, N])
        out_t = sb("out_t", [P, N])
        o_tok = sb("o_tok", [P, TT, HEADS * HD])
        o_feat = sb("o_feat", [P, 2, N])
        x1 = sb("x1", [P, TT, C])
        x1_norm = sb("x1_norm", [P, TT, C])
        h2T = sb("h2T", [P, 1 + N])
        shift_tmp = sb("shift_tmp", [P, 2, N])
        mixed = sb("mixed", [P, 2, N])
        k_relu = sb("k_relu", [P, N])
        k_act = sb("k_act", [P, N])
        tanh_r = sb("tanh_r", [P, N])
        rkv = sb("rkv", [P, TT, C])
        y = sb("y", [P, TT, C])
        w_qk = sb("w_qk", [P, 2, HEADS * HD])
        w_rest = sb("w_rest", [P, weights.shape[1]])
        wv = w_rest[:, 0:2 * C]
        wo = w_rest[:, 2 * C:4 * C].rearrange("p (a c) -> p a c", a=2)
        w_rkvT = w_rest[:, 4 * C:7 * C].rearrange("p (a c) -> p a c", a=3)
        mu = w_rest[:, 7 * C:7 * C + 2]
        wo_gated = sb("wo_gated", [P, 2, C])
        wvT_gated = sb("wvT_gated", [P, C])
        cond_wm = sb("cond_wm", [P, B + 6 * C])
        condT = cond_wm[:, 0:B]
        wm = cond_wm[:, B:B + 6 * C]
        tanh_c = sb("tanh_c", [P, B])
        silu_c = sb("silu_c", [P, B])
        silu_b = sb("silu_b", [P, B, P])
        mod_T = sb("mod_T", [P, 4, B])
        gates = sb("gates", [P, B, 2, C])
        gate_sign = sb("gate_sign", [P, 2, 2 * C])
        gate_size = sb("gate_size", [P, 2, 2 * C])
        mu_not = sb("mu_not", [P, 2])
        ident_f = sb("ident_f", [P, P])
        ident_b = sb("ident_b", [P, P], BF16)
        causal = sb("causal", [P, N])
        max_row = sb("max_row", [P, 2, GH, TT])
        max_rest = sb("max_rest", [P, GH, TT])
        max_rest2 = sb("max_rest2", [P, GH, TT])
        shift = sb("shift", [P, 2, PARTS, GH * TT], BF16)
        shift_T = sb("shift_T", [PARTS * GH * TT, 2, P], BF16)
        stats = sb("stats", [P, 2, TT, 6])
        mean_var = sb("mean_var", [P, 2, TT, 2])
        var_eps = sb("var_eps", [P, 2, TT])
        minus_half = sb("minus_half", [P, TT])
        rstd = sb("rstd", [P, 2, TT])
        denom_inv = sb("denom_inv", [P, TT, GH])

        st_bank = [ctx.enter_context(nc.psum_tensor(f"st{i}", [P, N], F32)) for i in range(ST)]
        sq_bank = [ctx.enter_context(nc.psum_tensor(f"sq{i}", [P, N], F32)) for i in range(SQ)]
        po_bank = ctx.enter_context(nc.psum_tensor("po", [P, N], F32))
        spare = [ctx.enter_context(nc.psum_tensor(f"spare{i}", [P, N], F32)) for i in range(2)]

        scratch = nc.dram_tensor("stacks_dram", [2, 2, len(Q_PARTS), 2, HD, GH, N], BF16).ap()

        st_ready = sem("st_ready")
        exp_done = sem("exp_done")
        sq_ready = sem("sq_ready")
        max_done = sem("max_done")
        dve_own = sem("dve_own")
        stats_done = sem("stats_done")
        pool_own = sem("pool_own")
        exps_seen = sem("exps_seen")
        stack_used = sem("stack_used")
        maxes_seen = sem("maxes_seen")
        shift_ready = sem("shift_ready")
        shift_loaded = [sem(f"shift_loaded{g}") for g in range(STEPS)]
        masked = sem("masked")
        po_ready = sem("po_ready")
        out_t_ready = sem("out_t_ready")
        ready = {u: sem(f"{u}_ready") for u in UNIT_AT}
        read = {u: sem(f"{u}_read") for u in UNIT_AT}
        hi_done = {u: sem(f"{u}_hi") for u in ("Q0", "K0", "Q1", "K1")}
        mid_done = {u: sem(f"{u}_mid") for u in ("Q0", "K0", "Q1", "K1")}
        lo_done = {u: sem(f"{u}_lo") for u in ("Q0", "K0", "Q1", "K1")}
        saved = [sem(f"saved{h}") for h in range(2)]
        stacked = [sem(f"stacked{g}") for g in range(STEPS)]
        x_loaded = sem("x_loaded")
        xres_loaded = sem("xres_loaded")
        norm_done = sem("norm_done")
        var_done = [sem(f"var_done{i}") for i in range(2)]
        rstd_done = [sem(f"rstd_done{i}") for i in range(2)]
        hTv_done = sem("hTv_done")
        o_tok_done = sem("o_tok_done")
        x1_norm_done = sem("x1_norm_done")
        mixture_half = sem("mixture_half")
        mixed_done = sem("mixed_done")
        relu_done = sem("relu_done")
        k_act_done = sem("k_act_done")
        wo_gated_done = sem("wo_gated_done")
        wv_gated_done = sem("wv_gated_done")
        y_done = sem("y_done")
        stored = sem("stored")
        passed = {e.engine: sem(f"passed_{n}") for n, e in
                  (("pe", nc.tensor), ("dve", nc.vector), ("pool", nc.gpsimd), ("sp", nc.sync))}
        s_cond = sem("s_cond")
        s_qk = sem("s_qk")
        s_w = sem("s_w")
        s_const = sem("s_const")
        s_tanh = sem("s_tanh")
        s_silu = sem("s_silu")
        s_silub = sem("s_silub")
        s_setup_pe = sem("s_setup_pe")
        s_mod = sem("s_mod")
        s_gate_units = sem("s_gate_units")
        s_gates = sem("s_gates")
        s_zero = sem("s_zero")
        s_ones = sem("s_ones")

        WRITES = 2 * len(BLOCK_RUNS)

        def works(b):
            return 0 <= b < B

        def taken(t):
            return min(max(t - LAG, 0), LOOP_END - LOOP_FIRST)

        def left(t, db, n):
            return UNITS * (t + db - taken(t)) + n

        def group_at(g, lag):
            return (g - lag) // STEPS, (g - lag) % STEPS

        def spare_at(g, slot, t):
            return [u for u in UNIT_AT if UNIT_AT[u][:2] == (g, slot) and works(t + UNIT_AT[u][2])]

        def bank_of(u):
            return po_bank if u in TURNS else spare[ORDER.index(u) % 2]

        def user_before(u, t):
            i, dt = ORDER.index(u), 0
            while t + dt >= FIRST:
                i -= 2
                if i < 0:
                    i, dt = i + len(ORDER), dt - 1
                v = ORDER[i]
                if works(t + dt + SPARE[v][2]):
                    return v, dt + SPARE[v][2]
            return None

        def apart(eng):
            eng.sem_inc(passed[eng.engine], 1)

        def iterations(eng, body):
            for t in range(FIRST, LOOP_FIRST):
                body(t, t)
            with eng.Fori(LOOP_FIRST, LOOP_END) as tv:
                body(LOOP_FIRST, tv)
            for t in range(LOOP_END, LAST + 1):
                body(t, t)

        block = ctx.enter_context(nc.Block())

        @block.sync
        def _(sp):
            sp.dma_start(x_in[:, :, :], x[0].rearrange("(t p) c -> p t c", p=P)).then_inc(x_loaded, 16)
            sp.dma_start(cond_wm[:, :], cond_mod).then_inc(s_cond, 16)
            sp.dma_start(w_qk[:, :, :].rearrange("p a c -> p (a c)"), qk_weights).then_inc(s_qk, 16)
            sp.dma_start(w_rest[:, :], weights).then_inc(s_w, 16)

            def stack_group(t, tv, db, g):
                sp.wait_ge(saved[g // 2], 16 * WRITES * (tv + db + 1))
                apart(sp)
                if works(t + db - 1):
                    sp.wait_ge(stack_used, STEPS * (tv + db - 1) + g + 1)
                for i, stack in enumerate((q_stack, k_stack)):
                    sp.dma_start(stack[0:STACK, g, :, :].rearrange("p h n -> p (h n)"),
                                 scratch[i, g // 2, :, g % 2].rearrange("s d h n -> s d (h n)")
                                 ).then_inc(stacked[g], 16)

            def load_shifts(t, tv, g):
                db, pg = group_at(g, 1)
                if not works(t + db):
                    return
                sp.wait_ge(read[f"MT{g}"], tv + db + 1)
                n = GH * TT
                for i in range(PARTS):
                    sp.dma_start(q_stack[STACK + i:STACK + i + 1, pg, :, :].rearrange("o h (q n) -> o (h q) n", n=P),
                                 shift_T[i * n:(i + 1) * n, pg % 2, :]).then_inc(shift_loaded[pg], 16)

            def save_half(t, tv, half):
                if works(t):
                    for g in (2 * half, 2 * half + 1):
                        sp.wait_ge(stacked[g], 16 * 2 * (tv + 1))
                for i, u in enumerate((f"Q{half}", f"K{half}")):
                    sp.wait_ge(lo_done[u], tv + 2)
                    for lo, hi in BLOCK_RUNS:
                        if i == 0:
                            src = parts[:, i, half, Q_PARTS[lo]:Q_PARTS[hi - 1] + 1, :]
                        else:
                            part = K_PARTS[lo]
                            src = parts[:, i, half, part:part + 1, :].to_broadcast([P, hi - lo, N])
                        sp.dma_start(scratch[i, half, lo:hi].rearrange("s g d h n -> (g d h) s n"),
                                     src).then_inc(saved[half], 16)

            def body(t, tv):
                for g in range(STEPS):
                    if g < STEPS - 1 and works(t):
                        stack_group(t, tv, 0, g + 1)
                    if g == STEPS - 1 and works(t + 1):
                        if t > FIRST:
                            stack_group(t, tv, 1, 0)
                    load_shifts(t, tv, g)
                    if g in (2, 3) and works(t + 1):
                        save_half(t, tv, g - 2)
                        if g == 2 and t == FIRST:
                            stack_group(t, tv, 1, 0)
                    if g == 0 and works(t - 1):
                        if works(t - 2):
                            sp.wait_ge(read["WO"], tv - 1)
                            apart(sp)
                        sp.dma_start(x_res[:, :, :], x[tv - 1].rearrange("(t p) c -> p t c", p=P)
                                     ).then_inc(xres_loaded, 16)
                    if g == 1 and works(t + 2):
                        sp.wait_ge(norm_done, tv + 2)
                        apart(sp)
                        sp.dma_start(x_in[:, :, :], x[tv + 2].rearrange("(t p) c -> p t c", p=P)
                                     ).then_inc(x_loaded, 16)
                    if g == 2 and works(t - 2):
                        sp.wait_ge(y_done, tv - 1)
                        apart(sp)
                        sp.dma_start(out[tv - 2].rearrange("(t p) c -> p t c", p=P), y[:, :, :]
                                     ).then_inc(stored, 16)

            iterations(sp, body)
            sp.wait_ge(stored, 16 * B)
            for h in range(2):
                sp.wait_ge(saved[h], 16 * WRITES * B)

        @block.tensor
        def _(pe):
            pe.wait_ge(s_silu, 1)
            for i, j in enumerate((0, 1, 3, 4)):
                last = nc.tensor.matmul(st_bank[1][:, i * B:(i + 1) * B], lhsT=wm[:, j * C:(j + 1) * C],
                                        rhs=silu_c[:, :], start=True, stop=True)
            last.then_inc(s_setup_pe, 1)
            pe.wait_ge(s_const, 1)

            def gate_unit(n):
                pe.wait_ge(s_silub, 1)
                if n:
                    pe.wait_ge(s_gates, n)
                for b in (2 * n, 2 * n + 1):
                    for i, j in enumerate((2, 5)):
                        at = (b % 2) * 2 * C + i * C
                        last = nc.tensor.matmul(po_bank[:, at:at + C], lhsT=silu_b[:, b, :],
                                                rhs=wm[:, j * C:(j + 1) * C], start=True, stop=True)
                last.then_inc(s_gate_units, 1)

            def p2_unit(t, tv, g, slot):
                db, pg = group_at(g, 2)
                if not works(t + db):
                    return
                h, j = divmod(slot, 3)
                if slot == 0:
                    pe.wait_ge(shift_loaded[pg], 48 * (tv + db + 1))
                unit = SLOTS * pg + slot
                if t + db == 0 and unit == 0:
                    pe.wait_ge(s_mod, 4)
                if UNITS * (t + db) + unit >= ST:
                    pe.wait_ge(exp_done, left(t, db, unit - ST + 1))
                ps = st_bank[slot % ST]
                for kb, at in (((0, 0),), ((1, 0),), ((2, 0), (3, 2 * P)))[j]:
                    last = nc.tensor.matmul(ps[:, at:at + N - kb * P],
                                            lhsT=k_stack[0:SHIFTED, pg, h, kb * P:(kb + 1) * P],
                                            rhs=q_stack[0:SHIFTED, pg, h, kb * P:N], start=True, stop=True)
                last.then_inc(st_ready, 1)

            def p1_unit(t, tv, g, slot):
                if not works(t):
                    return
                h, j = divmod(slot, 3)
                if slot == 0:
                    pe.wait_ge(stacked[g], 16 * 2 * (tv + 1))
                unit = SLOTS * g + slot
                if UNITS * t + unit >= SQ:
                    pe.wait_ge(max_done, left(t, 0, unit - SQ + 1))
                ps = sq_bank[slot % SQ]
                for qb, at in P1_BLOCKS[j]:
                    end = at + (qb + 1) * P
                    if slot == SLOTS - 1 and qb and works(t + group_at(g, 2)[0]):
                        last.then_inc(stack_used, 1)
                    last = nc.tensor.matmul(ps[:, at:end], lhsT=q_stack[0:STACK, g, h, qb * P:(qb + 1) * P],
                                            rhs=k_stack[0:STACK, g, h, 0:(qb + 1) * P], start=True, stop=True)
                last.then_inc(sq_ready, 1)

            def pv_block(t, tv, g, kb):
                db, pg = group_at(g, 3)
                if not works(t + db):
                    return
                if kb == 0:
                    if works(t - 1):
                        pe.wait_ge(read[f"OT{g}"], tv)
                    elif pg == 0:
                        pe.wait_ge(s_gates, B // 2)
                    pe.wait_ge(read["V1" if pg >= 2 else "V0"], tv + db + 1)
                pe.wait_ge(masked, TT * (STEPS * (tv + db) + pg) + kb + 1)
                for h in range(GH):
                    last = nc.tensor.matmul(po_bank[h * VW:(h + 1) * VW, kb * P:N],
                                            lhsT=v_ones[:, kb, pg * GH + h, :],
                                            rhs=probs[:, pg % 2, h, KB[kb]:KB[kb + 1]],
                                            start=kb == 0, stop=kb == TT - 1)
                if kb == TT - 1:
                    last.then_inc(po_ready, 1)

            def spare_unit(u, t, tv):
                g, _, db = UNIT_AT[u]
                b1 = tv + db + 1
                before = user_before(u, t) if u in SPARE else None
                if before:
                    pe.wait_ge(read[before[0]], tv + before[1] + 1)
                ps = bank_of(u)
                if u.startswith("OT"):
                    pe.wait_ge(out_t_ready, STEPS * (tv + db) + g + 1)
                    for i in range(TT):
                        last = nc.tensor.transpose(ps[:, i * P:(i + 1) * P], out_t[:, i * P:(i + 1) * P],
                                                   ident_f[:, :])
                elif u in ("HT", "H2T"):
                    pe.wait_ge(norm_done if u == "HT" else x1_norm_done, b1)
                    src = x_norm if u == "HT" else x1_norm
                    for i in range(TT):
                        last = nc.tensor.transpose(ps[:, i * P:(i + 1) * P], src[:, i, :], ident_f[:, :])
                elif u.startswith("MT"):
                    _, pg = group_at(g, 1)
                    pe.wait_ge(shift_ready, STEPS * (tv + db) + pg + 1)
                    apart(pe)
                    last = nc.tensor.transpose(ps[0:PARTS * GH * TT, 0:P // 2].bitcast(BF16),
                                               shift[:, pg % 2, :, :], ident_b[:, :])
                elif u[0] in "QK" and u[1] in "01":
                    half = int(u[1])
                    if t == FIRST:
                        pe.wait_ge(s_qk, 16)
                    pe.wait_ge(read["HT"], b1)
                    i = 0 if u[0] == "Q" else 1
                    last = nc.tensor.matmul(ps[:, :], lhsT=w_qk[:, i, half * P:(half + 1) * P], rhs=hT[:, :],
                                            start=True, stop=True)
                elif u in ("V0", "V1"):
                    half = int(u[1])
                    if t == 0 and half == 0:
                        pe.wait_ge(s_w, 16)
                    pe.wait_ge(hTv_done, b1)
                    for i in range(TT):
                        last = nc.tensor.matmul(ps[:, i * P:(i + 1) * P], lhsT=hT_v[:, i * P:(i + 1) * P],
                                                rhs=wv[:, half * P:(half + 1) * P], start=True, stop=True)
                elif u in ("OB0", "OB1"):
                    half = int(u[2])
                    pe.wait_ge(o_tok_done, STEPS * b1 if half else STEPS * (tv + db) + 2)
                    for i in range(TT):
                        last = nc.tensor.transpose(ps[:, i * P:(i + 1) * P],
                                                   o_tok[:, i, half * P:(half + 1) * P], ident_f[:, :])
                elif u == "WO":
                    pe.wait_ge(read["OB1"], b1)
                    pe.wait_ge(wo_gated_done, b1)
                    for i in range(TT):
                        for a in range(2):
                            last = nc.tensor.matmul(ps[:, i * P:(i + 1) * P],
                                                    lhsT=o_feat[:, a, i * P:(i + 1) * P],
                                                    rhs=wo_gated[:, a, :], start=a == 0, stop=a == 1)
                elif u == "KT":
                    pe.wait_ge(mixed_done, 2 * (tv + db) + 1)
                    last = nc.tensor.matmul(ps[:, :], lhsT=w_rkvT[:, 1, :], rhs=mixed[:, 1, :],
                                            start=True, stop=True)
                elif u == "R":
                    pe.wait_ge(mixed_done, 2 * b1)
                    for i in range(TT):
                        last = nc.tensor.matmul(ps[:, i * P:(i + 1) * P], lhsT=mixed[:, 0, i * P:(i + 1) * P],
                                                rhs=w_rkvT[:, 0, :], start=True, stop=True)
                elif u == "KV":
                    pe.wait_ge(k_act_done, b1)
                    pe.wait_ge(wv_gated_done, b1)
                    for i in range(TT):
                        last = nc.tensor.matmul(ps[:, i * P:(i + 1) * P], lhsT=k_act[:, i * P:(i + 1) * P],
                                                rhs=wvT_gated[:, :], start=True, stop=True)
                last.then_inc(ready[u], 1)

            def body(t, tv):
                for g in range(STEPS):
                    for slot in range(SLOTS):
                        p2_unit(t, tv, g, slot)
                        p1_unit(t, tv, g, slot)
                        if slot == ST - 1:
                            db, pg = group_at(g, 3)
                            if works(t + db):
                                if (works(t + group_at(g, 2)[0])) is False:
                                    pe.wait_ge(exp_done, left(t, db, SLOTS * (pg + 1)))
                                pe.sem_inc(exps_seen, 1)
                        if slot == SQ - 1:
                            db, pg = group_at(g, 1)
                            if works(t + db):
                                if not works(t):
                                    pe.wait_ge(max_done, left(t, db, SLOTS * (pg + 1)))
                                pe.sem_inc(maxes_seen, 1)
                        if t == 0 and (g, slot) in GATE_SLOTS:
                            gate_unit(GATE_SLOTS.index((g, slot)))
                        for u in spare_at(g, slot, t):
                            spare_unit(u, t, tv)
                        if PV_SLOT <= slot < PV_SLOT + TT:
                            pv_block(t, tv, g, slot - PV_SLOT)
                if t == LOOP_FIRST:
                    pe.sem_inc(exp_done, -UNITS)
                    pe.sem_inc(max_done, -UNITS)

            iterations(pe, body)

        @block.scalar
        def _(act):
            act.wait_ge(s_cond, 16)
            nc.scalar.activation(tanh_c[:, :], condT[:, :], ACT.Tanh, scale=0.5).then_inc(s_tanh, 1)

            def exp_unit(t, tv, g, slot):
                db, pg = group_at(g, 2)
                if not works(t + db):
                    return
                h, j = divmod(slot, 3)
                if slot == 0 and STEPS * (t + db) + pg >= 2:
                    act.wait_ge(po_ready, STEPS * (tv + db) + pg - 1)
                act.wait_ge(st_ready, left(t, db, SLOTS * pg + slot + 1))
                lo, hi = (KB[0], KB[1], KB[2], KB[4])[j:j + 2]
                nc.scalar.activation(probs[:, pg % 2, h, lo:hi], st_bank[slot % ST][:, 0:hi - lo], ACT.Exp,
                                     scale=SCALE).then_inc(exp_done, 1)

            def copy_out(t, tv, g):
                db, pg = group_at(g, 3)
                if not works(t + db):
                    return
                if STEPS * (t + db) + pg > 0:
                    act.wait_ge(ready[f"OT{(pg - 1) % STEPS}"], tv + db + (1 if pg else 0))
                act.wait_ge(po_ready, STEPS * (tv + db) + pg + 1)
                nc.scalar.copy(out_t[:, :], po_bank[:, :]).then_inc(out_t_ready, 1)

            def mixture_start(t, tv, i):
                if i == 1:
                    act.wait_ge(read["H2T"], tv - 1)
                    if t == LAG:
                        act.wait_ge(s_zero, 2)
                if works(t - 3):
                    act.wait_ge(mixed_done, 2 * (tv - 2) - i)
                nc.scalar.activation(shift_tmp[:, i, :], h2T[:, 0:N], ACT.Copy, scale=mu_not[:, i:i + 1]
                                     ).then_inc(mixture_half, 1)

            def copy_hT(t, tv):
                act.wait_ge(read["HT"], tv + 1)
                if works(t - 1):
                    act.wait_ge(ready["V1"], tv)
                nc.scalar.copy(hT_v[:, :], hT[:, :]).then_inc(hTv_done, 1)

            def spare_read(u, t, tv):
                g, _, db = UNIT_AT[u]
                b1 = tv + db + 1
                ps = bank_of(u)
                if u in ("H2T", "HT"):
                    act.wait_ge(ready[u], b1)
                    dst, i = (hT[:, :], 0) if u == "HT" else (h2T[:, 1:1 + N], 2)
                    if u == "HT":
                        act.wait_ge(s_mod, 4)
                        if works(t):
                            act.wait_ge(hTv_done, tv + 1)
                    elif works(t - 3):
                        act.wait_ge(mixed_done, 2 * (tv - 2))
                    b = bass.ds(tv + db, 1)
                    nc.scalar.activation(dst, ps[:, :], ACT.Identity, bias=mod_T[:, i, b],
                                         scale=mod_T[:, i + 1, b]).then_inc(read[u], 1)
                elif u.startswith("MT"):
                    act.wait_ge(ready[u], b1)
                    _, pg = group_at(g, 1)
                    if STEPS * (t + db) + pg >= 2:
                        sg, sdb = (pg - 2) % STEPS, db + (pg - 2) // STEPS
                        act.wait_ge(shift_loaded[sg], 48 * (tv + sdb + 1))
                    nc.scalar.copy(shift_T[:, pg % 2, :], ps[0:PARTS * GH * TT, 0:P // 2].bitcast(BF16)
                                   ).then_inc(read[u], 1)
                elif u == "KT":
                    act.wait_ge(ready[u], b1)
                    if works(t - 3):
                        act.wait_ge(k_act_done, tv - 2)
                    nc.scalar.activation(k_relu[:, :], ps[:, :], ACT.Relu).then_inc(read[u], 1)
                elif u[0] in "QK" and u[1] in "01":
                    half = int(u[1])
                    act.wait_ge(ready[u], b1)
                    if works(t):
                        act.wait_ge(saved[half], 16 * WRITES * (tv + 1))
                    nc.scalar.copy(parts[:, 0 if u[0] == "Q" else 1, half, 0, :], ps[:, :]
                                   ).then_inc(hi_done[u], 1)
                elif u == "R":
                    act.wait_ge(ready[u], b1)
                    if works(t - 3):
                        act.wait_ge(read["KV"], tv - 2)
                    nc.scalar.activation(tanh_r[:, :], ps[:, :], ACT.Tanh, scale=0.5).then_inc(read[u], 1)
                elif u in ("V0", "V1"):
                    half = int(u[1])
                    act.wait_ge(ready[u], b1)
                    if t == 0 and half == 0:
                        act.wait_ge(s_ones, 1)
                    hh = HEADS // 2
                    dst = v_ones[:, :, half * hh:(half + 1) * hh, 0:HD]
                    nc.scalar.copy(dst, ps[:, :].rearrange("p (t h d) -> p t h d", t=TT, d=HD)
                                   ).then_inc(read[u], 1)
                elif u in ("OB0", "OB1"):
                    half = int(u[2])
                    act.wait_ge(ready[u], b1)
                    if works(t - 2):
                        act.wait_ge(ready["WO"], tv - 1)
                    nc.scalar.copy(o_feat[:, half, :], ps[:, :]).then_inc(read[u], 1)

            def body(t, tv):
                for g in range(STEPS):
                    for slot in range(SLOTS + 1):
                        if slot == COPY_SLOT + 1:
                            copy_out(t, tv, g)
                        if slot < SLOTS:
                            exp_unit(t, tv, g, slot)
                        if g == 0 and slot == 1 and works(t):
                            copy_hT(t, tv)
                        if slot > 0:
                            for u in spare_at(g, slot - 1, t):
                                spare_read(u, t, tv)
                        if g == 0 and slot in (8, 10) and works(t - 2):
                            mixture_start(t, tv, int(slot == 8))
                if t == LOOP_FIRST:
                    act.sem_inc(st_ready, -UNITS)

            iterations(act, body)

        @block.vector
        def _(dve):
            def own(ins):
                ins.then_inc(dve_own, 1)
                dve.wait_ge(dve_own, 1)
                dve.sem_inc(dve_own, -1)

            def norm_stats(src, i, first):
                for a in (first, first + 1):
                    last = nc.vector.bn_stats(stats[:, i, a, :], src[:, a, :])
                if first:
                    last.then_inc(stats_done, 1)

            def norm_aggr(i):
                dve.wait_ge(stats_done, 1)
                dve.sem_inc(stats_done, -1)
                for a in range(TT):
                    last = nc.vector.bn_aggr(mean_var[:, i, a, :], stats[:, i, a, :])
                last.then_inc(var_done[i], 1)

            nc.vector.memset(h2T[:, 0:1], 0.0).then_inc(s_zero, 1)
            dve.wait_ge(x_loaded, 16)
            norm_stats(x_in, 0, 0)
            norm_stats(x_in, 0, 2)
            norm_aggr(0)
            dve.wait_ge(s_tanh, 1)
            own(nc.vector.scalar_tensor_tensor(out=tanh_c[:, :], in0=tanh_c[:, :], scalar=1.0,
                                               in1=condT[:, :], op0=ALU.add, op1=ALU.mult))
            nc.vector.tensor_scalar(silu_c[:, :], tanh_c[:, :], 0.5, None, ALU.mult).then_inc(s_silu, 1)
            dve.wait_ge(s_setup_pe, 1)
            for i in range(4):
                nc.vector.tensor_scalar(mod_T[:, i, :], st_bank[1][:, i * B:(i + 1) * B], float(i % 2), None,
                                        ALU.add).then_inc(s_mod, 1)

            def setup_rest():
                nc.vector.tensor_scalar(silu_b[:, :, :], tanh_c[:, :].unsqueeze(2).to_broadcast([P, B, P]),
                                        0.5, None, ALU.mult).then_inc(s_silub, 1)
                dve.wait_ge(s_w, 16)
                nc.vector.tensor_scalar(mu_not[:, :], mu[:, :], -1.0, 1.0, ALU.mult, ALU.add
                                        ).then_inc(s_zero, 1)

            def gate_read(n):
                dve.wait_ge(s_gate_units, n + 1)
                pair = po_bank[:, :].rearrange("p (b c) -> p b c", b=2)
                own(nc.vector.tensor_scalar(gate_sign[:, :, :], pair, 0.25, None, ALU.max))
                own(nc.vector.scalar_tensor_tensor(out=gate_size[:, :, :], in0=pair, scalar=-1.0,
                                                   in1=gate_sign[:, :, :], op0=ALU.mult, op1=ALU.max))
                own(nc.vector.tensor_scalar(gate_sign[:, :, :], pair, 0.0, 2.0, ALU.is_ge, ALU.mult))
                own(nc.vector.scalar_tensor_tensor(
                    out=gates[:, 2 * n:2 * n + 2, :, :].rearrange("p b a c -> p b (a c)"),
                    in0=gate_sign[:, :, :], scalar=-1.0, in1=gate_size[:, :, :],
                    op0=ALU.add, op1=ALU.mult))
                nc.vector.tensor_scalar(gates[:, 2 * n:2 * n + 2, 1, :], gates[:, 2 * n:2 * n + 2, 1, :],
                                        0.5, None, ALU.mult).then_inc(s_gates, 1)

            def max_unit(t, tv, g, slot):
                h, j = divmod(slot, 3)
                if slot == 0 and STEPS * t + g >= 2:
                    gg = STEPS * t + g - 1
                    dve.wait_ge(shift_ready, STEPS * tv + g - 1)
                    apart(dve)
                dve.wait_ge(sq_ready, left(t, 0, SLOTS * g + slot + 1))
                ps = sq_bank[slot % SQ]
                for qb, at in P1_BLOCKS[j]:
                    row = ps[:, at:at + (qb + 1) * P]
                    last = nc.vector.tensor_tensor_reduce(
                        out=row, in0=row, in1=causal[:, N - (qb + 1) * P:N], scale=1.0, scalar=LOWEST,
                        op0=ALU.add, op1=ALU.max, accum_out=max_row[:, g % 2, h, qb:qb + 1])
                last.then_inc(max_done, 1)

            def norm_apply(src, dst, i, done, b1):
                dve.wait_ge(rstd_done[i], b1)
                for a in range(TT):
                    last = nc.vector.tensor_scalar(dst[:, a, :], src[:, a, :], mean_var[:, i, a, 0:1],
                                                   rstd[:, i, a:a + 1], ALU.subtract, ALU.mult)
                last.then_inc(done, 1)

            def mixture_end(t, tv, i):
                dve.wait_ge(mixture_half, 2 * (tv - 1) - i)
                if works(t - 3):
                    dve.wait_ge(ready["KT" if i else "R"], tv - 2)
                nc.vector.scalar_tensor_tensor(out=mixed[:, i, :], in0=h2T[:, 1:1 + N],
                                               scalar=mu[:, i:i + 1], in1=shift_tmp[:, i, :],
                                               op0=ALU.mult, op1=ALU.add).then_inc(mixed_done, 1)

            def spare_read(u, t, tv):
                g, _, db = UNIT_AT[u]
                b1 = tv + db + 1
                ps = bank_of(u)
                if u.startswith("OT"):
                    dve.wait_ge(ready[u], b1)
                    if g == 0 and works(t - 2):
                        dve.wait_ge(ready["OB1"], tv - 1)
                    o = ps[:, :].rearrange("p (t h w) -> p t h w", t=TT, w=VW)
                    own(nc.vector.reciprocal(denom_inv[:, :, :], o[:, :, :, HD]))
                    dst = o_tok[:, :, g * GH * HD:(g + 1) * GH * HD].rearrange("p t (h d) -> p t h d", d=HD)
                    nc.vector.tensor_tensor(dst, o[:, :, :, 0:HD],
                                            denom_inv[:, :, :].unsqueeze(3).to_broadcast([P, TT, GH, HD]),
                                            ALU.mult).then_inc(read[u], 1)
                    dve.wait_ge(read[u], b1)
                    dve.sem_inc(o_tok_done, 1)
                elif u[0] in "QK" and u[1] in "01":
                    i, half = (0 if u[0] == "Q" else 1), int(u[1])
                    dve.wait_ge(hi_done[u], b1)
                    if half:
                        dve.wait_ge(lo_done[u[0] + "0"], b1)
                    elif works(t):
                        dve.wait_ge(lo_done[u[0] + "1"], tv + 1)
                    nc.vector.tensor_tensor(rest[:, i, :], ps[:, :], parts[:, i, half, 0, :], ALU.subtract
                                            ).then_inc(read[u], 1)
                    dve.wait_ge(read[u], b1)
                    nc.vector.tensor_copy(parts[:, i, half, 1, :], rest[:, i, :]).then_inc(mid_done[u], 1)
                elif u == "WO":
                    dve.wait_ge(ready[u], b1)
                    dve.wait_ge(xres_loaded, 16 * b1)
                    if works(t - 2):
                        dve.wait_ge(y_done, tv - 1)
                    nc.vector.tensor_tensor(x1[:, :, :], ps[:, :].rearrange("p (t c) -> p t c", t=TT),
                                            x_res[:, :, :], ALU.add).then_inc(read[u], 1)
                    dve.wait_ge(read[u], b1)
                    norm_stats(x1, 1, 0)
                    norm_stats(x1, 1, 2)
                elif u == "KV":
                    dve.wait_ge(ready[u], b1)
                    dve.wait_ge(read["R"], b1)
                    if works(t - 3):
                        dve.wait_ge(y_done, tv - 2)
                    nc.vector.scalar_tensor_tensor(out=rkv[:, :, :],
                                                   in0=tanh_r[:, :].rearrange("p (t c) -> p t c", t=TT),
                                                   scalar=1.0, in1=ps[:, :].rearrange("p (t c) -> p t c", t=TT),
                                                   op0=ALU.add, op1=ALU.mult).then_inc(read[u], 1)

            def body(t, tv):
                for g in range(STEPS):
                    for slot in range(SLOTS + 1):
                        if slot < SLOTS and works(t):
                            max_unit(t, tv, g, slot)
                        if g == 3 and works(t + 2):
                            if slot == 0:
                                dve.wait_ge(x_loaded, 16 * (tv + 3))
                                norm_stats(x_in, 0, 0)
                            elif slot == 1:
                                norm_stats(x_in, 0, 2)
                            elif slot == 2:
                                norm_aggr(0)
                            elif slot == 8:
                                if works(t + 1):
                                    dve.wait_ge(ready["HT"], tv + 2)
                                norm_apply(x_in, x_norm, 0, norm_done, tv + 3)
                        if g == 0 and works(t - 2):
                            if slot == 1:
                                if works(t - 3):
                                    dve.wait_ge(ready["H2T"], tv - 2)
                                norm_apply(x1, x1_norm, 1, x1_norm_done, tv - 1)
                            elif slot in (9, 11):
                                mixture_end(t, tv, int(slot == 9))
                        if t == 0 and (g, slot - 1) in GATE_SLOTS:
                            gate_read(GATE_SLOTS.index((g, slot - 1)))
                        if slot > 0:
                            for u in spare_at(g, slot - 1, t):
                                spare_read(u, t, tv)
                        if g == STEPS - 1 and slot == 10 and works(t - 1):
                            norm_aggr(1)
                    if t == FIRST and g == 2:
                        setup_rest()
                if t == LOOP_FIRST:
                    dve.sem_inc(sq_ready, -UNITS)

            norm_apply(x_in, x_norm, 0, norm_done, 1)
            iterations(dve, body)

        @block.gpsimd
        def _(pool):
            def own(ins):
                ins.then_inc(pool_own, 1)
                pool.wait_ge(pool_own, 1)
                pool.sem_inc(pool_own, -1)

            own(nc.gpsimd.memset(minus_half[:, :], -0.5))
            own(nc.gpsimd.memset(ident_f[:, :], 0.0))
            own(nc.gpsimd.memset(ident_b[:, :], 0.0))
            own(nc.gpsimd.memset(causal[:, :], 0.0))
            nc.gpsimd.affine_select(out=causal[:, N - P:N], in_=causal[:, N - P:N], compare_op=ALU.is_ge, fill=MASKED,
                                    base=0, pattern=[[-1, P]], channel_multiplier=1)
            nc.gpsimd.affine_select(out=ident_b[:, :], in_=ident_b[:, :], compare_op=ALU.not_equal, fill=1.0,
                                    base=0, pattern=[[-1, P]], channel_multiplier=1)
            nc.gpsimd.affine_select(out=ident_f[:, :], in_=ident_f[:, :], compare_op=ALU.not_equal, fill=1.0,
                                    base=0, pattern=[[-1, P]], channel_multiplier=1).then_inc(s_const, 1)

            def shift_rows(t, tv, g):
                db, pg = group_at(g, 1)
                if not works(t + db):
                    return
                b = pg % 2
                pool.wait_ge(maxes_seen, STEPS * (tv + db) + pg + 1)
                apart(pool)
                own(nc.gpsimd.tensor_scalar(shift[:, b, 0, :].rearrange("p (h q) -> p h q", q=TT),
                                            max_row[:, b, :, :], -1.0, None, ALU.mult))
                own(nc.gpsimd.tensor_tensor(max_rest[:, :, :], max_row[:, b, :, :],
                                            shift[:, b, 0, :].rearrange("p (h q) -> p h q", q=TT), ALU.add))
                own(nc.gpsimd.tensor_scalar(shift[:, b, 1, :].rearrange("p (h q) -> p h q", q=TT),
                                            max_rest[:, :, :], -1.0, None, ALU.mult))
                own(nc.gpsimd.tensor_tensor(max_rest2[:, :, :], max_rest[:, :, :],
                                            shift[:, b, 1, :].rearrange("p (h q) -> p h q", q=TT), ALU.add))
                nc.gpsimd.tensor_scalar(shift[:, b, 2, :].rearrange("p (h q) -> p h q", q=TT),
                                        max_rest2[:, :, :], -1.0, None, ALU.mult).then_inc(shift_ready, 1)

            def mask_probs(t, tv, g, kbs):
                db, pg = group_at(g, 3)
                if not works(t + db):
                    return
                if kbs[0] == 0:
                    pool.wait_ge(exps_seen, STEPS * (tv + db) + pg + 1)
                    apart(pool)
                for kb in kbs:
                    d = probs[:, pg % 2, :, KB[kb]:KB[kb] + P]
                    nc.gpsimd.affine_select(out=d, in_=d, compare_op=ALU.is_ge, fill=0.0, base=0,
                                            pattern=[[0, GH], [1, P]], channel_multiplier=-1
                                            ).then_inc(masked, 1)

            def inverse_std(i, b1):
                pool.wait_ge(var_done[i], b1)
                apart(pool)
                own(nc.gpsimd.tensor_scalar(var_eps[:, i, :], mean_var[:, i, :, 1], EPS, None, ALU.add))
                nc.gpsimd.tensor_tensor(rstd[:, i, :], var_eps[:, i, :], minus_half[:, :], ALU.pow
                                        ).then_inc(rstd_done[i], 1)

            def low_part(t, tv, u):
                i, half = (0 if u[0] == "Q" else 1), int(u[1])
                pool.wait_ge(mid_done[u], tv + 2)
                nc.gpsimd.tensor_tensor(parts[:, i, half, 2, :], rest[:, i, :], parts[:, i, half, 1, :],
                                        ALU.subtract).then_inc(lo_done[u], 1)

            def body(t, tv):
                for g in range(STEPS):
                    mask_probs(t, tv, g, (0,))
                    shift_rows(t, tv, g)
                    mask_probs(t, tv, g, range(1, TT))
                    if g == 3 and works(t + 2):
                        inverse_std(0, tv + 3)
                    if g == 0 and works(t - 1):
                        if t == 1:
                            pool.wait_ge(s_gates, B // 2)
                            pool.wait_ge(s_w, 16)
                        if works(t - 2):
                            pool.wait_ge(ready["WO"], tv - 1)
                        nc.gpsimd.tensor_tensor(wo_gated[:, :, :], wo[:, :, :],
                                                gates[:, bass.ds(tv - 1, 1), 0, :].to_broadcast([P, 2, C]),
                                                ALU.mult).then_inc(wo_gated_done, 1)
                    if g == 0 and works(t - 2):
                        if works(t - 3):
                            pool.wait_ge(ready["KV"], tv - 2)
                        nc.gpsimd.tensor_tensor(wvT_gated[:, :], w_rkvT[:, 2, :],
                                                gates[:, bass.ds(tv - 2, 1), 1, :].squeeze(1),
                                                ALU.mult).then_inc(wv_gated_done, 1)
                    if g == 1 and works(t - 2):
                        pool.wait_ge(read["KT"], tv - 1)
                        if works(t - 3):
                            pool.wait_ge(ready["KV"], tv - 2)
                        nc.gpsimd.tensor_tensor(k_act[:, :], k_relu[:, :], k_relu[:, :], ALU.mult
                                                ).then_inc(k_act_done, 1)
                    if g >= 2 and works(t + 1):
                        low_part(t, tv, f"K{g - 2}")
                    if g in (1, 2) and works(t + 1):
                        low_part(t, tv, f"Q{g - 1}")
                    if g == 2 and works(t - 2):
                        pool.wait_ge(read["KV"], tv - 1)
                        if works(t - 3):
                            pool.wait_ge(stored, 16 * (tv - 2))
                        nc.gpsimd.tensor_tensor(y[:, :, :], rkv[:, :, :], x1[:, :, :], ALU.add
                                                ).then_inc(y_done, 1)
                    if g == STEPS - 1 and works(t - 1):
                        inverse_std(1, tv)
                    if g == STEPS - 1 and t == FIRST:
                        pool.wait_ge(lo_done["K1"], 1)
                        pool.wait_ge(rstd_done[0], 2)
                        own(nc.gpsimd.memset(k_stack[STACK:P, :, :, :], 1.0))
                        nc.gpsimd.memset(v_ones[:, :, :, HD:VW], 1.0).then_inc(s_ones, 1)

            inverse_std(0, 1)
            iterations(pool, body)


def kernel(**inputs):
    import numpy as _np
    import concourse.bacc as _bacc
    from concourse import mybir as _mybir
    from concourse.bass_utils import run_bass_kernel_spmd as _run

    a = {name: _np.asarray(v) for name, v in inputs.items()}

    def by_channel(w):
        return w.reshape(w.shape[0], STEPS, GH, HD).transpose(0, 1, 3, 2).reshape(w.shape)

    layout = {
        "x": a["L0_attn_x"],
        "cond_mod": _np.concatenate([a["L0_c"].T, a["L0_wmod"]], axis=1),
        "qk_weights": _np.concatenate([by_channel(a["L0_attn_Wq"]), by_channel(a["L0_attn_Wk"])], axis=1),
        "weights": _np.concatenate([a["L0_attn_Wv"], a["L0_attn_Wo"][:P], a["L0_attn_Wo"][P:],
                                    a["L0_ffn_W_r"].T, a["L0_ffn_W_k"].T, a["L0_ffn_W_v"].T,
                                    a["L0_ffn_mu_r"][:, None], a["L0_ffn_mu_k"][:, None]], axis=1),
    }
    nc = _bacc.Bacc("TRN2", target_bir_lowering=False, num_devices=1)
    arrays, args = {}, []
    for name, v in layout.items():
        v = _np.ascontiguousarray(v)
        arrays[f"in_{name}_dram"] = v
        args.append(nc.dram_tensor(f"in_{name}_dram", v.shape, _mybir.dt.from_np(v.dtype), kind="ExternalInput").ap())
    args.append(nc.dram_tensor("out_0_dram", a["L0_attn_x"].shape, _mybir.dt.float32, kind="ExternalOutput").ap())
    build(nc, *args)
    r = _run(nc, [arrays], core_ids=[0])
    return r.results[0]["out_0_dram"]
```

```python
from contextlib import ExitStack

import concourse.bass as bass
from concourse import mybir

F32 = mybir.dt.float32
BF16 = mybir.dt.bfloat16
ALU = mybir.AluOpType
ACT = mybir.ActivationFunctionType

P = 128
HEADS = 16
HD = 16
GH = 4
STEPS = HEADS // GH
SLOTS = 12
UNITS = SLOTS * STEPS
ST, SQ = 2, 3
PARTS = 3
Q_PARTS = (0, 1, 2, 0, 1, 0)
K_PARTS = (0, 0, 0, 1, 1, 2)
BLOCK_RUNS = ((0, 3), (3, 5), (5, 6))
STACK = HD * len(Q_PARTS)
SHIFTED = STACK + PARTS
VW = 32
MASKED = -1.0e30
LOWEST = -3.0e38
SCALE = float((HD // 2) ** -0.5)
EPS = 1e-5

SPARE = {
    "V1": (0, 1, -1), "HT": (0, 3, 1), "MT0": (0, 6, -1), "H2T": (0, 6, -2),
    "KT": (1, 0, -2), "R": (1, 1, -2), "Q0": (1, 4, 1), "MT1": (1, 5, 0), "K0": (1, 11, 1),
    "KV": (2, 0, -2), "V0": (2, 3, 0), "Q1": (2, 5, 1), "MT2": (2, 5, 0), "K1": (2, 11, 1),
    "OB0": (3, 2, -1), "MT3": (3, 5, 0), "OB1": (3, 6, -1), "WO": (3, 8, -1),
}
ORDER = list(SPARE)
TURN_SLOTS = (2, 2, 1, 1)
TURNS = {f"OT{g}": (g, TURN_SLOTS[g], -1) for g in range(STEPS)}
UNIT_AT = {**TURNS, **SPARE}

PV_SLOT = 7
COPY_SLOT = 11
MAXES_SLOT = 2
MASKS_FIRST = (1, 0, 1, 1)
READ_LAG = {'Q0': 2, 'K0': 1, 'Q1': 2, 'K1': 1, 'KV': 1, 'WO': 1}
NORM_X = (3, (2, 6, 7, 10, 12))
NORM_1 = (10, (2, 3))
MIX_START = (8, 9)
MIX_END = (9, 11)
COPY_HT = 0
MID_LAG = 3
MID_AT = {divmod(g * SLOTS + slot + MID_LAG, SLOTS): u
          for u, (g, slot, _) in SPARE.items() if u in ("Q0", "K0", "Q1", "K1")}
P1_BLOCKS = (((3, 0),), ((2, 0),), ((0, 0), (1, P)))
LOOP_FIRST, LAG = 2, 2


def build(nc, x, cond_mod, qk_weights, weights, out):
    B, N, C = x.shape
    TT = N // P
    assert C == P and TT == 4 and qk_weights.shape[1] == 2 * HEADS * HD
    LOOP_END = B - 2
    FIRST, LAST = -1, B + 1
    KB = [0]
    for kb in range(TT):
        KB.append(KB[-1] + N - kb * P)
    PROB = KB[TT]

    with ExitStack() as ctx:
        def sb(name, shape, dt=F32):
            return ctx.enter_context(nc.sbuf_tensor(name, shape, dt))

        def sem(name):
            return ctx.enter_context(nc.semaphore(name))

        q_stack = sb("q_stack", [P, STEPS, GH, N], BF16)
        k_stack = sb("k_stack", [P, STEPS, GH, N], BF16)
        probs = sb("probs", [P, 2, GH, PROB])
        v_ones = sb("v_ones", [P, TT, HEADS, VW])
        parts = sb("parts", [P, 2, 2, PARTS, N], BF16)
        rest = sb("rest", [P, 2, N])
        x_in = sb("x_in", [P, TT, C])
        x_res = sb("x_res", [P, TT, C])
        x_norm = sb("x_norm", [P, TT, C])
        hT = sb("hT", [P, N])
        hT_v = sb("hT_v", [P, N])
        out_t = sb("out_t", [P, N])
        o_tok = sb("o_tok", [P, TT, HEADS * HD])
        o_feat = sb("o_feat", [P, 2, N])
        x1 = sb("x1", [P, TT, C])
        x1_norm = sb("x1_norm", [P, TT, C])
        h2T = sb("h2T", [P, 1 + N])
        shift_tmp = sb("shift_tmp", [P, 2, N])
        mixed = sb("mixed", [P, 2, N])
        k_relu = sb("k_relu", [P, N])
        k_act = sb("k_act", [P, N])
        tanh_r = sb("tanh_r", [P, N])
        rkv = sb("rkv", [P, TT, C])
        y = sb("y", [P, TT, C])
        w_qk = sb("w_qk", [P, 2, HEADS * HD])
        w_rest = sb("w_rest", [P, weights.shape[1]])
        wv = w_rest[:, 0:2 * C]
        wo = w_rest[:, 2 * C:4 * C].rearrange("p (a c) -> p a c", a=2)
        w_rkvT = w_rest[:, 4 * C:7 * C].rearrange("p (a c) -> p a c", a=3)
        mu = w_rest[:, 7 * C:7 * C + 2]
        wo_gated = sb("wo_gated", [P, 2, C])
        wvT_gated = sb("wvT_gated", [P, C])
        cond_wm = sb("cond_wm", [P, B + 6 * C])
        condT = cond_wm[:, 0:B]
        wm = cond_wm[:, B:B + 6 * C]
        tanh_c = sb("tanh_c", [P, B])
        silu_c = sb("silu_c", [P, B])
        gate_T = sb("gate_T", [P, B, 2])
        gate_wide = sb("gate_wide", [P, 2 * B, P])
        mod_T = sb("mod_T", [P, 4, B])
        gates = sb("gates", [P, B, 2, C])
        gate_sign = sb("gate_sign", [P, 2, B])
        gate_size = sb("gate_size", [P, 2, B])
        mu_not = sb("mu_not", [P, 2])
        ident_f = sb("ident_f", [P, P])
        ident_b = sb("ident_b", [P, P], BF16)
        causal = sb("causal", [P, N])
        max_row = sb("max_row", [P, 2, GH, TT])
        max_rest = sb("max_rest", [P, GH, TT])
        max_rest2 = sb("max_rest2", [P, GH, TT])
        shift = sb("shift", [P, 2, PARTS, GH * TT], BF16)
        shift_T = sb("shift_T", [PARTS * GH * TT, 2, P], BF16)
        stats = sb("stats", [P, 2, TT, 6])
        mean_var = sb("mean_var", [P, 2, TT, 2])
        var_eps = sb("var_eps", [P, 2, TT])
        minus_half = sb("minus_half", [P, TT])
        rstd = sb("rstd", [P, 2, TT])
        denom_inv = sb("denom_inv", [P, TT, GH])

        st_bank = [ctx.enter_context(nc.psum_tensor(f"st{i}", [P, N], F32)) for i in range(ST)]
        sq_bank = [ctx.enter_context(nc.psum_tensor(f"sq{i}", [P, N], F32)) for i in range(SQ)]
        po_bank = ctx.enter_context(nc.psum_tensor("po", [P, N], F32))
        spare = [ctx.enter_context(nc.psum_tensor(f"spare{i}", [P, N], F32)) for i in range(2)]

        scratch = nc.dram_tensor("stacks_dram", [2, 2, len(Q_PARTS), 2, HD, GH, N], BF16).ap()

        st_ready = sem("st_ready")
        exp_done = sem("exp_done")
        sq_ready = sem("sq_ready")
        max_done = sem("max_done")
        dve_own = sem("dve_own")
        denoms_done = sem("denoms_done")
        stats_done = sem("stats_done")
        pool_own = sem("pool_own")
        exps_seen = sem("exps_seen")
        stack_used = sem("stack_used")
        maxes_seen = sem("maxes_seen")
        shift_ready = sem("shift_ready")
        shift_loaded = [sem(f"shift_loaded{g}") for g in range(STEPS)]
        masked = sem("masked")
        po_ready = sem("po_ready")
        out_t_ready = sem("out_t_ready")
        ready = {u: sem(f"{u}_ready") for u in UNIT_AT}
        read = {u: sem(f"{u}_read") for u in UNIT_AT}
        hi_done = {u: sem(f"{u}_hi") for u in ("Q0", "K0", "Q1", "K1")}
        mid_done = {u: sem(f"{u}_mid") for u in ("Q0", "K0", "Q1", "K1")}
        lo_done = {u: sem(f"{u}_lo") for u in ("Q0", "K0", "Q1", "K1")}
        saved = [sem(f"saved{h}") for h in range(2)]
        stacked = [sem(f"stacked{g}") for g in range(STEPS)]
        x_loaded = sem("x_loaded")
        xres_loaded = sem("xres_loaded")
        norm_done = sem("norm_done")
        var_done = [sem(f"var_done{i}") for i in range(2)]
        rstd_done = [sem(f"rstd_done{i}") for i in range(2)]
        hTv_done = sem("hTv_done")
        x1_norm_done = sem("x1_norm_done")
        mixture_half = sem("mixture_half")
        mixed_done = sem("mixed_done")
        k_act_done = sem("k_act_done")
        wo_gated_done = sem("wo_gated_done")
        wv_gated_done = sem("wv_gated_done")
        y_done = sem("y_done")
        stored = sem("stored")
        passed = {e.engine: sem(f"passed_{n}") for n, e in
                  (("pe", nc.tensor), ("dve", nc.vector), ("pool", nc.gpsimd), ("sp", nc.sync))}
        s_cond = sem("s_cond")
        s_qk = sem("s_qk")
        s_w = sem("s_w")
        s_const = sem("s_const")
        s_tanh = sem("s_tanh")
        s_silu = sem("s_silu")
        s_setup_pe = sem("s_setup_pe")
        s_mod = sem("s_mod")
        s_gate_T = sem("s_gate_T")
        s_gate_units = sem("s_gate_units")
        s_gates = sem("s_gates")
        s_zero = sem("s_zero")
        s_ones = sem("s_ones")
        s_first_stack = [sem(f"s_first_stack{g}") for g in range(2)]

        WRITES = 2 * len(BLOCK_RUNS)

        def works(b):
            return 0 <= b < B

        def taken(t):
            return min(max(t - LAG, 0), LOOP_END - LOOP_FIRST)

        def left(t, db, n):
            return UNITS * (t + db - taken(t)) + n

        def group_at(g, lag):
            return (g - lag) // STEPS, (g - lag) % STEPS

        def spare_at(g, slot, t):
            return [u for u in UNIT_AT if UNIT_AT[u][:2] == (g, slot) and works(t + UNIT_AT[u][2])]

        START_BANK = {"K0": sq_bank[0], "K1": st_bank[0]}
        gate_bank = (sq_bank[1], sq_bank[2], po_bank, st_bank[1])

        def read_at(g, slot, t):
            return [u for u in UNIT_AT if works(t + UNIT_AT[u][2])
                    and (UNIT_AT[u][0], UNIT_AT[u][1] + READ_LAG.get(u, 1)) == (g, slot)]

        def bank_of(u, t):
            if t == FIRST and u in START_BANK:
                return START_BANK[u]
            return po_bank if u in TURNS else spare[ORDER.index(u) % 2]

        def user_before(u, t):
            i, dt = ORDER.index(u), 0
            while t + dt >= FIRST:
                i -= 2
                if i < 0:
                    i, dt = i + len(ORDER), dt - 1
                v = ORDER[i]
                if works(t + dt + SPARE[v][2]) and bank_of(v, t + dt) in spare:
                    return v, dt + SPARE[v][2]
            return None

        def apart(eng):
            eng.sem_inc(passed[eng.engine], 1)

        def iterations(eng, body):
            for t in range(FIRST, LOOP_FIRST):
                body(t, t)
            with eng.Fori(LOOP_FIRST, LOOP_END) as tv:
                body(LOOP_FIRST, tv)
            for t in range(LOOP_END, LAST + 1):
                body(t, t)

        block = ctx.enter_context(nc.Block())

        @block.sync
        def _(sp):
            sp.dma_start(x_in[:, :, :], x[0].rearrange("(t p) c -> p t c", p=P)).then_inc(x_loaded, 16)
            sp.dma_start(cond_wm[:, :], cond_mod).then_inc(s_cond, 16)
            sp.dma_start(w_qk[:, :, :].rearrange("p a c -> p (a c)"), qk_weights).then_inc(s_qk, 16)
            sp.dma_start(w_rest[:, :], weights).then_inc(s_w, 16)

            def first_stack(g):
                for i, (u, stack, which) in enumerate((("Q0", q_stack, Q_PARTS), ("K0", k_stack, K_PARTS))):
                    for part, done in enumerate((hi_done[u], mid_done[u], lo_done[u])):
                        sp.wait_ge(done, 1)
                        for s in range(len(which)):
                            if which[s] == part:
                                sp.dma_start(stack[s * HD:(s + 1) * HD, g, :, :],
                                             parts[g * HD * GH:(g + 1) * HD * GH, i, 0, part, :]
                                             ).then_inc(s_first_stack[g], 16)

            def stack_group(t, tv, db, g):
                sp.wait_ge(saved[g // 2], 16 * WRITES * (tv + db + 1))
                apart(sp)
                if works(t + db - 1):
                    sp.wait_ge(stack_used, STEPS * (tv + db - 1) + g + 1)
                for i, stack in enumerate((q_stack, k_stack)):
                    sp.dma_start(stack[0:STACK, g, :, :].rearrange("p h n -> p (h n)"),
                                 scratch[i, g // 2, :, g % 2].rearrange("s d h n -> s d (h n)")
                                 ).then_inc(stacked[g], 16)

            def load_shifts(t, tv, g):
                db, pg = group_at(g, 1)
                if not works(t + db):
                    return
                sp.wait_ge(read[f"MT{g}"], tv + db + 1)
                n = GH * TT
                for i in range(PARTS):
                    sp.dma_start(q_stack[STACK + i:STACK + i + 1, pg, :, :].rearrange("o h (q n) -> o (h q) n", n=P),
                                 shift_T[i * n:(i + 1) * n, pg % 2, :]).then_inc(shift_loaded[pg], 16)

            def save_half(t, tv, half):
                if works(t):
                    for g in (2 * half, 2 * half + 1):
                        sp.wait_ge(stacked[g], 16 * 2 * (tv + 1))
                for i, u in enumerate((f"Q{half}", f"K{half}")):
                    sp.wait_ge(lo_done[u], tv + 2)
                    for lo, hi in BLOCK_RUNS:
                        if i == 0:
                            src = parts[:, i, half, Q_PARTS[lo]:Q_PARTS[hi - 1] + 1, :]
                        else:
                            part = K_PARTS[lo]
                            src = parts[:, i, half, part:part + 1, :].to_broadcast([P, hi - lo, N])
                        sp.dma_start(scratch[i, half, lo:hi].rearrange("s g d h n -> (g d h) s n"),
                                     src).then_inc(saved[half], 16)

            def body(t, tv):
                for g in range(STEPS):
                    if g < STEPS - 1 and works(t) and (t, g) != (0, 0):
                        stack_group(t, tv, 0, g + 1)
                    if g == STEPS - 1 and works(t + 1):
                        if t > FIRST:
                            stack_group(t, tv, 1, 0)
                    load_shifts(t, tv, g)
                    if g == 2 and t == FIRST:
                        first_stack(0)
                        first_stack(1)
                    elif g in (2, 3) and works(t + 1):
                        save_half(t, tv, g - 2)
                    if g == STEPS - 1 and t == FIRST:
                        for group in range(2):
                            sp.wait_ge(s_first_stack[group], 16 * 2 * len(Q_PARTS))
                            sp.sem_inc(stacked[group], 16 * 2)
                        sp.sem_inc(saved[0], 16 * WRITES)
                    if g == 0 and works(t - 1):
                        if works(t - 2):
                            sp.wait_ge(read["WO"], tv - 1)
                            apart(sp)
                        sp.dma_start(x_res[:, :, :], x[tv - 1].rearrange("(t p) c -> p t c", p=P)
                                     ).then_inc(xres_loaded, 16)
                    if g == 1 and works(t + 2):
                        sp.wait_ge(norm_done, tv + 2)
                        apart(sp)
                        sp.dma_start(x_in[:, :, :], x[tv + 2].rearrange("(t p) c -> p t c", p=P)
                                     ).then_inc(x_loaded, 16)
                    if g == 2 and works(t - 2):
                        sp.wait_ge(y_done, tv - 1)
                        apart(sp)
                        sp.dma_start(out[tv - 2].rearrange("(t p) c -> p t c", p=P), y[:, :, :]
                                     ).then_inc(stored, 16)

            iterations(sp, body)
            sp.wait_ge(stored, 16 * B)
            for h in range(2):
                sp.wait_ge(saved[h], 16 * WRITES * B)

        @block.tensor
        def _(pe):
            pe.wait_ge(s_silu, 1)
            for i, j in enumerate((0, 1, 3, 4, 2, 5)):
                last = nc.tensor.matmul(st_bank[1][:, i * B:(i + 1) * B], lhsT=wm[:, j * C:(j + 1) * C],
                                        rhs=silu_c[:, :], start=True, stop=True)
            last.then_inc(s_setup_pe, 1)
            pe.wait_ge(s_const, 1)

            def gate_units():
                pe.wait_ge(s_gate_T, 1)
                for n, bank in enumerate(gate_bank):
                    for i in range(4):
                        last = nc.tensor.matmul(bank[:, i * C:(i + 1) * C], lhsT=gate_wide[:, 4 * n + i, :],
                                                rhs=ident_f[:, :], start=True, stop=True)
                    last.then_inc(s_gate_units, 1)

            def p2_unit(t, tv, g, slot):
                db, pg = group_at(g, 2)
                if not works(t + db):
                    return
                h, j = divmod(slot, 3)
                if slot == 0:
                    pe.wait_ge(shift_loaded[pg], 48 * (tv + db + 1))
                unit = SLOTS * pg + slot
                if UNITS * (t + db) + unit >= ST:
                    pe.wait_ge(exp_done, left(t, db, unit - ST + 1))
                ps = st_bank[slot % ST]
                for kb, at in (((0, 0),), ((1, 0),), ((2, 0), (3, 2 * P)))[j]:
                    last = nc.tensor.matmul(ps[:, at:at + N - kb * P],
                                            lhsT=k_stack[0:SHIFTED, pg, h, kb * P:(kb + 1) * P],
                                            rhs=q_stack[0:SHIFTED, pg, h, kb * P:N], start=True, stop=True)
                last.then_inc(st_ready, 1)

            def p1_unit(t, tv, g, slot):
                if not works(t):
                    return
                h, j = divmod(slot, 3)
                if t == 0 and g == 0 and slot == 0:
                    pe.wait_ge(s_gates, len(gate_bank))
                    pe.wait_ge(read["K1"], 1)
                    pe.wait_ge(s_first_stack[0], 16 * 2 * len(Q_PARTS))
                elif slot == 0:
                    pe.wait_ge(stacked[g], 16 * 2 * (tv + 1))
                unit = SLOTS * g + slot
                if UNITS * t + unit >= SQ:
                    pe.wait_ge(max_done, left(t, 0, unit - SQ + 1))
                ps = sq_bank[slot % SQ]
                for qb, at in P1_BLOCKS[j]:
                    end = at + (qb + 1) * P
                    if slot == SLOTS - 1 and qb and works(t + group_at(g, 2)[0]):
                        last.then_inc(stack_used, 1)
                    last = nc.tensor.matmul(ps[:, at:end], lhsT=q_stack[0:STACK, g, h, qb * P:(qb + 1) * P],
                                            rhs=k_stack[0:STACK, g, h, 0:(qb + 1) * P], start=True, stop=True)
                last.then_inc(sq_ready, 1)

            def pv_block(t, tv, g, kb):
                db, pg = group_at(g, 3)
                if not works(t + db):
                    return
                if kb == 0:
                    if works(t - 1):
                        pe.wait_ge(read[f"OT{g}"], tv)
                    pe.wait_ge(read["V1" if pg >= 2 else "V0"], tv + db + 1)
                pe.wait_ge(masked, TT * (STEPS * (tv + db) + pg) + kb + 1)
                for h in range(GH):
                    last = nc.tensor.matmul(po_bank[h * VW:(h + 1) * VW, kb * P:N],
                                            lhsT=v_ones[:, kb, pg * GH + h, :],
                                            rhs=probs[:, pg % 2, h, KB[kb]:KB[kb + 1]],
                                            start=kb == 0, stop=kb == TT - 1)
                if kb == TT - 1:
                    last.then_inc(po_ready, 1)

            def spare_unit(u, t, tv):
                g, _, db = UNIT_AT[u]
                b1 = tv + db + 1
                before = user_before(u, t) if u in SPARE and bank_of(u, t) in spare else None
                if before:
                    pe.wait_ge(read[before[0]], tv + before[1] + 1)
                ps = bank_of(u, t)
                if u.startswith("OT"):
                    pe.wait_ge(out_t_ready, STEPS * (tv + db) + g + 1)
                    for i in range(TT):
                        last = nc.tensor.transpose(ps[:, i * P:(i + 1) * P], out_t[:, i * P:(i + 1) * P],
                                                   ident_f[:, :])
                elif u in ("HT", "H2T"):
                    pe.wait_ge(norm_done if u == "HT" else x1_norm_done, b1)
                    src = x_norm if u == "HT" else x1_norm
                    for i in range(TT):
                        last = nc.tensor.transpose(ps[:, i * P:(i + 1) * P], src[:, i, :], ident_f[:, :])
                elif u.startswith("MT"):
                    _, pg = group_at(g, 1)
                    pe.wait_ge(shift_ready, STEPS * (tv + db) + pg + 1)
                    apart(pe)
                    last = nc.tensor.transpose(ps[0:PARTS * GH * TT, 0:P // 2].bitcast(BF16),
                                               shift[:, pg % 2, :, :], ident_b[:, :])
                elif u[0] in "QK" and u[1] in "01":
                    half = int(u[1])
                    if t == FIRST:
                        pe.wait_ge(s_qk, 16)
                    pe.wait_ge(read["HT"], b1)
                    i = 0 if u[0] == "Q" else 1
                    last = nc.tensor.matmul(ps[:, :], lhsT=w_qk[:, i, half * P:(half + 1) * P], rhs=hT[:, :],
                                            start=True, stop=True)
                elif u in ("V0", "V1"):
                    half = int(u[1])
                    if t == 0 and half == 0:
                        pe.wait_ge(s_w, 16)
                    pe.wait_ge(hTv_done, b1)
                    for i in range(TT):
                        last = nc.tensor.matmul(ps[:, i * P:(i + 1) * P], lhsT=hT_v[:, i * P:(i + 1) * P],
                                                rhs=wv[:, half * P:(half + 1) * P], start=True, stop=True)
                elif u in ("OB0", "OB1"):
                    half = int(u[2])
                    pe.wait_ge(read["OT3" if half else "OT1"], b1)
                    for i in range(TT):
                        last = nc.tensor.transpose(ps[:, i * P:(i + 1) * P],
                                                   o_tok[:, i, half * P:(half + 1) * P], ident_f[:, :])
                elif u == "WO":
                    pe.wait_ge(read["OB1"], b1)
                    pe.wait_ge(wo_gated_done, b1)
                    for i in range(TT):
                        for a in range(2):
                            last = nc.tensor.matmul(ps[:, i * P:(i + 1) * P],
                                                    lhsT=o_feat[:, a, i * P:(i + 1) * P],
                                                    rhs=wo_gated[:, a, :], start=a == 0, stop=a == 1)
                elif u == "KT":
                    pe.wait_ge(mixed_done, 2 * (tv + db) + 1)
                    last = nc.tensor.matmul(ps[:, :], lhsT=w_rkvT[:, 1, :], rhs=mixed[:, 1, :],
                                            start=True, stop=True)
                elif u == "R":
                    pe.wait_ge(mixed_done, 2 * b1)
                    for i in range(TT):
                        last = nc.tensor.matmul(ps[:, i * P:(i + 1) * P], lhsT=mixed[:, 0, i * P:(i + 1) * P],
                                                rhs=w_rkvT[:, 0, :], start=True, stop=True)
                elif u == "KV":
                    pe.wait_ge(k_act_done, b1)
                    pe.wait_ge(wv_gated_done, b1)
                    for i in range(TT):
                        last = nc.tensor.matmul(ps[:, i * P:(i + 1) * P], lhsT=k_act[:, i * P:(i + 1) * P],
                                                rhs=wvT_gated[:, :], start=True, stop=True)
                last.then_inc(ready[u], 1)

            def body(t, tv):
                for g in range(STEPS):
                    for slot in range(SLOTS):
                        p2_unit(t, tv, g, slot)
                        p1_unit(t, tv, g, slot)
                        if slot == ST - 1:
                            db, pg = group_at(g, 3)
                            if works(t + db):
                                if (works(t + group_at(g, 2)[0])) is False:
                                    pe.wait_ge(exp_done, left(t, db, SLOTS * (pg + 1)))
                                pe.sem_inc(exps_seen, 1)
                        if slot == MAXES_SLOT:
                            db, pg = group_at(g, 1)
                            if works(t + db):
                                if not works(t) or MAXES_SLOT < SQ - 1:
                                    pe.wait_ge(max_done, left(t, db, SLOTS * (pg + 1)))
                                pe.sem_inc(maxes_seen, 1)
                        for u in spare_at(g, slot, t):
                            spare_unit(u, t, tv)
                        if t == FIRST and (g, slot) == SPARE["K1"][:2]:
                            gate_units()
                        if PV_SLOT <= slot < PV_SLOT + TT:
                            pv_block(t, tv, g, slot - PV_SLOT)
                if t == LOOP_FIRST:
                    pe.sem_inc(exp_done, -UNITS)
                    pe.sem_inc(max_done, -UNITS)

            iterations(pe, body)

        @block.scalar
        def _(act):
            act.wait_ge(s_cond, 16)
            nc.scalar.activation(tanh_c[:, :], condT[:, :], ACT.Tanh, scale=0.5).then_inc(s_tanh, 1)

            def exp_unit(t, tv, g, slot):
                db, pg = group_at(g, 2)
                if not works(t + db):
                    return
                h, j = divmod(slot, 3)
                if slot == 0 and STEPS * (t + db) + pg >= 2:
                    act.wait_ge(po_ready, STEPS * (tv + db) + pg - 1)
                act.wait_ge(st_ready, left(t, db, SLOTS * pg + slot + 1))
                lo, hi = (KB[0], KB[1], KB[2], KB[4])[j:j + 2]
                nc.scalar.activation(probs[:, pg % 2, h, lo:hi], st_bank[slot % ST][:, 0:hi - lo], ACT.Exp,
                                     scale=SCALE).then_inc(exp_done, 1)

            def gate_reads():
                for n, bank in enumerate(gate_bank):
                    act.wait_ge(s_gate_units, n + 1)
                    nc.scalar.copy(gates[:, 2 * n:2 * n + 2, :, :].rearrange("p b i c -> p (b i c)"), bank[:, :]
                                   ).then_inc(s_gates, 1)

            def copy_out(t, tv, g):
                db, pg = group_at(g, 3)
                if not works(t + db):
                    return
                if STEPS * (t + db) + pg > 0:
                    act.wait_ge(ready[f"OT{(pg - 1) % STEPS}"], tv + db + (1 if pg else 0))
                act.wait_ge(po_ready, STEPS * (tv + db) + pg + 1)
                nc.scalar.copy(out_t[:, :], po_bank[:, :]).then_inc(out_t_ready, 1)

            def mixture_start(t, tv, i):
                if i == 1:
                    act.wait_ge(read["H2T"], tv - 1)
                    if t == LAG:
                        act.wait_ge(s_zero, 2)
                if works(t - 3):
                    act.wait_ge(mixed_done, 2 * (tv - 2) - i)
                nc.scalar.activation(shift_tmp[:, i, :], h2T[:, 0:N], ACT.Copy, scale=mu_not[:, i:i + 1]
                                     ).then_inc(mixture_half, 1)

            def copy_hT(t, tv):
                act.wait_ge(read["HT"], tv + 1)
                if works(t - 1):
                    act.wait_ge(ready["V1"], tv)
                nc.scalar.copy(hT_v[:, :], hT[:, :]).then_inc(hTv_done, 1)

            def spare_read(u, t, tv):
                g, _, db = UNIT_AT[u]
                b1 = tv + db + 1
                ps = bank_of(u, t)
                if u in ("H2T", "HT"):
                    act.wait_ge(ready[u], b1)
                    dst, i = (hT[:, :], 0) if u == "HT" else (h2T[:, 1:1 + N], 2)
                    if u == "HT":
                        act.wait_ge(s_mod, 4)
                        if works(t):
                            act.wait_ge(hTv_done, tv + 1)
                    elif works(t - 3):
                        act.wait_ge(mixed_done, 2 * (tv - 2))
                    b = bass.ds(tv + db, 1)
                    nc.scalar.activation(dst, ps[:, :], ACT.Identity, bias=mod_T[:, i, b],
                                         scale=mod_T[:, i + 1, b]).then_inc(read[u], 1)
                elif u.startswith("MT"):
                    act.wait_ge(ready[u], b1)
                    _, pg = group_at(g, 1)
                    if STEPS * (t + db) + pg >= 2:
                        sg, sdb = (pg - 2) % STEPS, db + (pg - 2) // STEPS
                        act.wait_ge(shift_loaded[sg], 48 * (tv + sdb + 1))
                    nc.scalar.copy(shift_T[:, pg % 2, :], ps[0:PARTS * GH * TT, 0:P // 2].bitcast(BF16)
                                   ).then_inc(read[u], 1)
                elif u == "KT":
                    act.wait_ge(ready[u], b1)
                    if works(t - 3):
                        act.wait_ge(k_act_done, tv - 2)
                    nc.scalar.activation(k_relu[:, :], ps[:, :], ACT.Relu).then_inc(read[u], 1)
                elif u[0] in "QK" and u[1] in "01":
                    half = int(u[1])
                    act.wait_ge(ready[u], b1)
                    if works(t):
                        act.wait_ge(saved[half], 16 * WRITES * (tv + 1))
                    nc.scalar.copy(parts[:, 0 if u[0] == "Q" else 1, half, 0, :], ps[:, :]
                                   ).then_inc(hi_done[u], 1)
                elif u == "R":
                    act.wait_ge(ready[u], b1)
                    if works(t - 3):
                        act.wait_ge(read["KV"], tv - 2)
                    nc.scalar.activation(tanh_r[:, :], ps[:, :], ACT.Tanh, scale=0.5).then_inc(read[u], 1)
                elif u in ("V0", "V1"):
                    half = int(u[1])
                    act.wait_ge(ready[u], b1)
                    if t == 0 and half == 0:
                        act.wait_ge(s_ones, 1)
                    hh = HEADS // 2
                    dst = v_ones[:, :, half * hh:(half + 1) * hh, 0:HD]
                    nc.scalar.copy(dst, ps[:, :].rearrange("p (t h d) -> p t h d", t=TT, d=HD)
                                   ).then_inc(read[u], 1)
                elif u in ("OB0", "OB1"):
                    half = int(u[2])
                    act.wait_ge(ready[u], b1)
                    if works(t - 2):
                        act.wait_ge(ready["WO"], tv - 1)
                    nc.scalar.copy(o_feat[:, half, :], ps[:, :]).then_inc(read[u], 1)

            def mid_part(t, tv, u):
                i, half = (0 if u[0] == "Q" else 1), int(u[1])
                act.wait_ge(read[u], tv + 2)
                nc.scalar.copy(parts[:, i, half, 1, :], rest[:, i, :]).then_inc(mid_done[u], 1)

            def body(t, tv):
                for g in range(STEPS):
                    for slot in range(SLOTS + 1):
                        if slot == COPY_SLOT + 1:
                            copy_out(t, tv, g)
                        if slot < SLOTS:
                            exp_unit(t, tv, g, slot)
                        if g == 0 and slot == COPY_HT and works(t):
                            copy_hT(t, tv)
                        if slot > 0:
                            for u in spare_at(g, slot - 1, t):
                                spare_read(u, t, tv)
                            if t == FIRST and (g, slot - 1) == SPARE["K1"][:2]:
                                gate_reads()
                        if (g, slot) in MID_AT and works(t + 1):
                            mid_part(t, tv, MID_AT[g, slot])
                        if g == 0 and slot in MIX_START and works(t - 2):
                            mixture_start(t, tv, 1 - MIX_START.index(slot))
                if t == LOOP_FIRST:
                    act.sem_inc(st_ready, -UNITS)

            iterations(act, body)

        @block.vector
        def _(dve):
            def own(ins):
                ins.then_inc(dve_own, 1)
                dve.wait_ge(dve_own, 1)
                dve.sem_inc(dve_own, -1)

            def norm_stats(src, i, first):
                for a in (first, first + 1):
                    last = nc.vector.bn_stats(stats[:, i, a, :], src[:, a, :])
                if first:
                    last.then_inc(stats_done, 1)

            def norm_aggr(i):
                dve.wait_ge(stats_done, 1)
                dve.sem_inc(stats_done, -1)
                for a in range(TT):
                    last = nc.vector.bn_aggr(mean_var[:, i, a, :], stats[:, i, a, :])
                last.then_inc(var_done[i], 1)

            def norm_apply(src, dst, i, done, b1, tiles=range(TT)):
                if tiles[0] == 0:
                    dve.wait_ge(rstd_done[i], b1)
                for a in tiles:
                    last = nc.vector.tensor_scalar(dst[:, a, :], src[:, a, :], mean_var[:, i, a, 0:1],
                                                   rstd[:, i, a:a + 1], ALU.subtract, ALU.mult)
                if tiles[-1] == TT - 1:
                    last.then_inc(done, 1)

            nc.vector.memset(h2T[:, 0:1], 0.0).then_inc(s_zero, 1)
            dve.wait_ge(x_loaded, 16)
            norm_stats(x_in, 0, 0)
            norm_stats(x_in, 0, 2)
            norm_aggr(0)
            dve.wait_ge(s_tanh, 1)
            own(nc.vector.scalar_tensor_tensor(out=tanh_c[:, :], in0=tanh_c[:, :], scalar=1.0,
                                               in1=condT[:, :], op0=ALU.add, op1=ALU.mult))
            nc.vector.tensor_scalar(silu_c[:, :], tanh_c[:, :], 0.5, None, ALU.mult).then_inc(s_silu, 1)
            norm_apply(x_in, x_norm, 0, norm_done, 1)
            dve.wait_ge(s_setup_pe, 1)
            for i in range(4):
                nc.vector.tensor_scalar(mod_T[:, i, :], st_bank[1][:, i * B:(i + 1) * B], float(i % 2), None,
                                        ALU.add).then_inc(s_mod, 1)

            def make_gates():
                raw = st_bank[1][:, 4 * B:6 * B].rearrange("p (i b) -> p i b", i=2)
                own(nc.vector.tensor_scalar(gate_sign[:, :, :], raw, 0.25, None, ALU.max))
                own(nc.vector.scalar_tensor_tensor(out=gate_size[:, :, :], in0=raw, scalar=-1.0,
                                                   in1=gate_sign[:, :, :], op0=ALU.mult, op1=ALU.max))
                own(nc.vector.tensor_scalar(gate_sign[:, :, :], raw, 0.0, 2.0, ALU.is_ge, ALU.mult))
                own(nc.vector.scalar_tensor_tensor(out=gate_T[:, :, :].rearrange("p b i -> p i b"),
                                                   in0=gate_sign[:, :, :], scalar=-1.0, in1=gate_size[:, :, :],
                                                   op0=ALU.add, op1=ALU.mult))
                own(nc.vector.tensor_scalar(gate_T[:, :, 1:2], gate_T[:, :, 1:2], 0.5, None, ALU.mult))
                wide = gate_T[:, :, :].rearrange("p b i -> p (b i)").unsqueeze(2).to_broadcast([P, 2 * B, P])
                nc.vector.tensor_copy(gate_wide[:, :, :], wide).then_inc(s_gate_T, 1)
                dve.wait_ge(s_w, 16)
                nc.vector.tensor_scalar(mu_not[:, :], mu[:, :], -1.0, 1.0, ALU.mult, ALU.add
                                        ).then_inc(s_zero, 1)

            def max_unit(t, tv, g, slot):
                h, j = divmod(slot, 3)
                if slot == 0 and STEPS * t + g >= 2:
                    gg = STEPS * t + g - 1
                    dve.wait_ge(shift_ready, STEPS * tv + g - 1)
                    apart(dve)
                dve.wait_ge(sq_ready, left(t, 0, SLOTS * g + slot + 1))
                ps = sq_bank[slot % SQ]
                for qb, at in P1_BLOCKS[j]:
                    row = ps[:, at:at + (qb + 1) * P]
                    last = nc.vector.tensor_tensor_reduce(
                        out=row, in0=row, in1=causal[:, N - (qb + 1) * P:N], scale=1.0, scalar=LOWEST,
                        op0=ALU.add, op1=ALU.max, accum_out=max_row[:, g % 2, h, qb:qb + 1])
                last.then_inc(max_done, 1)

            def mixture_end(t, tv, i):
                dve.wait_ge(mixture_half, 2 * (tv - 1) - i)
                if works(t - 3):
                    dve.wait_ge(ready["KT" if i else "R"], tv - 2)
                nc.vector.scalar_tensor_tensor(out=mixed[:, i, :], in0=h2T[:, 1:1 + N],
                                               scalar=mu[:, i:i + 1], in1=shift_tmp[:, i, :],
                                               op0=ALU.mult, op1=ALU.add).then_inc(mixed_done, 1)

            def spare_read(u, t, tv, part=0):
                g, _, db = UNIT_AT[u]
                b1 = tv + db + 1
                ps = bank_of(u, t)
                if u.startswith("OT"):
                    if part == 0:
                        dve.wait_ge(ready[u], b1)
                        if g == 0 and works(t - 2):
                            dve.wait_ge(ready["OB1"], tv - 1)
                    o = ps[:, :].rearrange("p (t h w) -> p t h w", t=TT, w=VW)
                    if part == 0:
                        nc.vector.reciprocal(denom_inv[:, :, :], o[:, :, :, HD]).then_inc(denoms_done, 1)
                        return
                    dve.wait_ge(denoms_done, 1)
                    dve.sem_inc(denoms_done, -1)
                    dst = o_tok[:, :, g * GH * HD:(g + 1) * GH * HD].rearrange("p t (h d) -> p t h d", d=HD)
                    nc.vector.tensor_tensor(dst, o[:, :, :, 0:HD],
                                            denom_inv[:, :, :].unsqueeze(3).to_broadcast([P, TT, GH, HD]),
                                            ALU.mult).then_inc(read[u], 1)
                elif u[0] in "QK" and u[1] in "01":
                    i, half = (0 if u[0] == "Q" else 1), int(u[1])
                    dve.wait_ge(hi_done[u], b1)
                    if half:
                        dve.wait_ge(lo_done[u[0] + "0"], b1)
                    elif works(t):
                        dve.wait_ge(lo_done[u[0] + "1"], tv + 1)
                    nc.vector.tensor_tensor(rest[:, i, :], ps[:, :], parts[:, i, half, 0, :], ALU.subtract
                                            ).then_inc(read[u], 1)
                elif u == "WO":
                    dve.wait_ge(ready[u], b1)
                    dve.wait_ge(xres_loaded, 16 * b1)
                    if works(t - 2):
                        dve.wait_ge(y_done, tv - 1)
                    nc.vector.tensor_tensor(x1[:, :, :], ps[:, :].rearrange("p (t c) -> p t c", t=TT),
                                            x_res[:, :, :], ALU.add).then_inc(read[u], 1)
                    dve.wait_ge(read[u], b1)
                    norm_stats(x1, 1, 0)
                    norm_stats(x1, 1, 2)
                elif u == "KV":
                    dve.wait_ge(ready[u], b1)
                    dve.wait_ge(read["R"], b1)
                    if works(t - 3):
                        dve.wait_ge(y_done, tv - 2)
                    nc.vector.scalar_tensor_tensor(out=rkv[:, :, :],
                                                   in0=tanh_r[:, :].rearrange("p (t c) -> p t c", t=TT),
                                                   scalar=1.0, in1=ps[:, :].rearrange("p (t c) -> p t c", t=TT),
                                                   op0=ALU.add, op1=ALU.mult).then_inc(read[u], 1)

            def body(t, tv):
                for g in range(STEPS):
                    for slot in range(SLOTS + 1):
                        if slot < SLOTS and works(t):
                            max_unit(t, tv, g, slot)
                        if g == NORM_X[0] and works(t + 2):
                            if slot == NORM_X[1][0]:
                                dve.wait_ge(x_loaded, 16 * (tv + 3))
                                norm_stats(x_in, 0, 0)
                            if slot == NORM_X[1][1]:
                                norm_stats(x_in, 0, 2)
                            if slot == NORM_X[1][2]:
                                norm_aggr(0)
                            if slot == NORM_X[1][3]:
                                if works(t + 1):
                                    dve.wait_ge(ready["HT"], tv + 2)
                                norm_apply(x_in, x_norm, 0, norm_done, tv + 3, range(0, 2))
                            if slot == NORM_X[1][4]:
                                norm_apply(x_in, x_norm, 0, norm_done, tv + 3, range(2, TT))
                        if g == 0 and works(t - 2):
                            if slot == NORM_1[1][0]:
                                if works(t - 3):
                                    dve.wait_ge(ready["H2T"], tv - 2)
                                norm_apply(x1, x1_norm, 1, x1_norm_done, tv - 1, range(0, 2))
                            if slot == NORM_1[1][1]:
                                norm_apply(x1, x1_norm, 1, x1_norm_done, tv - 1, range(2, TT))
                            if slot in MIX_END:
                                mixture_end(t, tv, 1 - MIX_END.index(slot))
                        for u in read_at(g, slot, t):
                            spare_read(u, t, tv)
                        if slot > 1:
                            for u in spare_at(g, slot - 2, t):
                                if u in TURNS:
                                    spare_read(u, t, tv, part=1)
                        if g == STEPS - 1 and slot == NORM_1[0] and works(t - 1):
                            norm_aggr(1)
                    if t == LAST and g == 1:
                        dve.wait_ge(read["KT"], B)
                        dve.wait_ge(ready["KV"], B - 1)
                        nc.vector.tensor_tensor(k_act[:, :], k_relu[:, :], k_relu[:, :], ALU.mult
                                                ).then_inc(k_act_done, 1)
                    if t == LAST and g == 2:
                        dve.wait_ge(read["KV"], B)
                        dve.wait_ge(stored, 16 * (B - 1))
                        nc.vector.tensor_tensor(y[:, :, :], rkv[:, :, :], x1[:, :, :], ALU.add
                                                ).then_inc(y_done, 1)
                if t == LOOP_FIRST:
                    dve.sem_inc(sq_ready, -UNITS)

            make_gates()
            iterations(dve, body)

        @block.gpsimd
        def _(pool):
            def own(ins):
                ins.then_inc(pool_own, 1)
                pool.wait_ge(pool_own, 1)
                pool.sem_inc(pool_own, -1)

            own(nc.gpsimd.memset(minus_half[:, :], -0.5))
            own(nc.gpsimd.memset(ident_f[:, :], 0.0))
            own(nc.gpsimd.memset(ident_b[:, :], 0.0))
            own(nc.gpsimd.memset(causal[:, :], 0.0))
            nc.gpsimd.affine_select(out=causal[:, N - P:N], in_=causal[:, N - P:N], compare_op=ALU.is_ge, fill=MASKED,
                                    base=0, pattern=[[-1, P]], channel_multiplier=1)
            nc.gpsimd.affine_select(out=ident_b[:, :], in_=ident_b[:, :], compare_op=ALU.not_equal, fill=1.0,
                                    base=0, pattern=[[-1, P]], channel_multiplier=1)
            nc.gpsimd.affine_select(out=ident_f[:, :], in_=ident_f[:, :], compare_op=ALU.not_equal, fill=1.0,
                                    base=0, pattern=[[-1, P]], channel_multiplier=1).then_inc(s_const, 1)

            def shift_rows(t, tv, g):
                db, pg = group_at(g, 1)
                if not works(t + db):
                    return
                b = pg % 2
                pool.wait_ge(maxes_seen, STEPS * (tv + db) + pg + 1)
                apart(pool)
                own(nc.gpsimd.tensor_scalar(shift[:, b, 0, :].rearrange("p (h q) -> p h q", q=TT),
                                            max_row[:, b, :, :], -1.0, None, ALU.mult))
                own(nc.gpsimd.tensor_tensor(max_rest[:, :, :], max_row[:, b, :, :],
                                            shift[:, b, 0, :].rearrange("p (h q) -> p h q", q=TT), ALU.add))
                own(nc.gpsimd.tensor_scalar(shift[:, b, 1, :].rearrange("p (h q) -> p h q", q=TT),
                                            max_rest[:, :, :], -1.0, None, ALU.mult))
                own(nc.gpsimd.tensor_tensor(max_rest2[:, :, :], max_rest[:, :, :],
                                            shift[:, b, 1, :].rearrange("p (h q) -> p h q", q=TT), ALU.add))
                nc.gpsimd.tensor_scalar(shift[:, b, 2, :].rearrange("p (h q) -> p h q", q=TT),
                                        max_rest2[:, :, :], -1.0, None, ALU.mult).then_inc(shift_ready, 1)

            def mask_probs(t, tv, g, kbs):
                db, pg = group_at(g, 3)
                if not works(t + db):
                    return
                if 0 in kbs:
                    pool.wait_ge(exps_seen, STEPS * (tv + db) + pg + 1)
                    apart(pool)
                for kb in kbs:
                    d = probs[:, pg % 2, :, KB[kb]:KB[kb] + P]
                    nc.gpsimd.affine_select(out=d, in_=d, compare_op=ALU.is_ge, fill=0.0, base=0,
                                            pattern=[[0, GH], [1, P]], channel_multiplier=-1
                                            ).then_inc(masked, 1)

            def inverse_std(i, b1):
                pool.wait_ge(var_done[i], b1)
                apart(pool)
                own(nc.gpsimd.tensor_scalar(var_eps[:, i, :], mean_var[:, i, :, 1], EPS, None, ALU.add))
                nc.gpsimd.tensor_tensor(rstd[:, i, :], var_eps[:, i, :], minus_half[:, :], ALU.pow
                                        ).then_inc(rstd_done[i], 1)

            def low_part(t, tv, u):
                i, half = (0 if u[0] == "Q" else 1), int(u[1])
                pool.wait_ge(mid_done[u], tv + 2)
                nc.gpsimd.tensor_tensor(parts[:, i, half, 2, :], rest[:, i, :], parts[:, i, half, 1, :],
                                        ALU.subtract).then_inc(lo_done[u], 1)

            def body(t, tv):
                for g in range(STEPS):
                    mask_probs(t, tv, g, range(MASKS_FIRST[g]))
                    shift_rows(t, tv, g)
                    mask_probs(t, tv, g, range(MASKS_FIRST[g], TT))
                    if g == 0 and works(t - 1):
                        if t == 1:
                            pool.wait_ge(s_gates, len(gate_bank))
                            pool.wait_ge(s_w, 16)
                        if works(t - 2):
                            pool.wait_ge(ready["WO"], tv - 1)
                        nc.gpsimd.tensor_tensor(wo_gated[:, :, :], wo[:, :, :],
                                                gates[:, bass.ds(tv - 1, 1), 0, :].to_broadcast([P, 2, C]),
                                                ALU.mult).then_inc(wo_gated_done, 1)
                    if g == 0 and works(t - 2):
                        if works(t - 3):
                            pool.wait_ge(ready["KV"], tv - 2)
                        nc.gpsimd.tensor_tensor(wvT_gated[:, :], w_rkvT[:, 2, :],
                                                gates[:, bass.ds(tv - 2, 1), 1, :].squeeze(1),
                                                ALU.mult).then_inc(wv_gated_done, 1)
                    if g == 1 and works(t - 2) and t < LAST:
                        pool.wait_ge(read["KT"], tv - 1)
                        if works(t - 3):
                            pool.wait_ge(ready["KV"], tv - 2)
                        nc.gpsimd.tensor_tensor(k_act[:, :], k_relu[:, :], k_relu[:, :], ALU.mult
                                                ).then_inc(k_act_done, 1)
                    if g == NORM_X[0] and t == FIRST:
                        inverse_std(0, tv + 3)
                    if g >= 2 and works(t + 1):
                        low_part(t, tv, f"K{g - 2}")
                    if g in (1, 2) and works(t + 1):
                        low_part(t, tv, f"Q{g - 1}")
                    if g == 2 and works(t - 2) and t < LAST:
                        pool.wait_ge(read["KV"], tv - 1)
                        if works(t - 3):
                            pool.wait_ge(stored, 16 * (tv - 2))
                        nc.gpsimd.tensor_tensor(y[:, :, :], rkv[:, :, :], x1[:, :, :], ALU.add
                                                ).then_inc(y_done, 1)
                    if g == NORM_X[0] and FIRST < t and works(t + 2):
                        inverse_std(0, tv + 3)
                    if g == STEPS - 1 and works(t - 1):
                        inverse_std(1, tv)
            inverse_std(0, 1)
            pool.wait_ge(rstd_done[0], 1)
            own(nc.gpsimd.memset(k_stack[STACK:P, :, :, :], 1.0))
            nc.gpsimd.memset(v_ones[:, :, :, HD:VW], 1.0).then_inc(s_ones, 1)
            iterations(pool, body)


def kernel(**inputs):
    import numpy as _np
    import concourse.bacc as _bacc
    from concourse import mybir as _mybir
    from concourse.bass_utils import run_bass_kernel_spmd as _run

    a = {name: _np.asarray(v) for name, v in inputs.items()}

    def by_channel(w):
        return w.reshape(w.shape[0], STEPS, GH, HD).transpose(0, 1, 3, 2).reshape(w.shape)

    layout = {
        "x": a["L0_attn_x"],
        "cond_mod": _np.concatenate([a["L0_c"].T, a["L0_wmod"]], axis=1),
        "qk_weights": _np.concatenate([by_channel(a["L0_attn_Wq"]), by_channel(a["L0_attn_Wk"])], axis=1),
        "weights": _np.concatenate([a["L0_attn_Wv"], a["L0_attn_Wo"][:P], a["L0_attn_Wo"][P:],
                                    a["L0_ffn_W_r"].T, a["L0_ffn_W_k"].T, a["L0_ffn_W_v"].T,
                                    a["L0_ffn_mu_r"][:, None], a["L0_ffn_mu_k"][:, None]], axis=1),
    }
    nc = _bacc.Bacc("TRN2", target_bir_lowering=False, num_devices=1)
    arrays, args = {}, []
    for name, v in layout.items():
        v = _np.ascontiguousarray(v)
        arrays[f"in_{name}_dram"] = v
        args.append(nc.dram_tensor(f"in_{name}_dram", v.shape, _mybir.dt.from_np(v.dtype), kind="ExternalInput").ap())
    args.append(nc.dram_tensor("out_0_dram", a["L0_attn_x"].shape, _mybir.dt.float32, kind="ExternalOutput").ap())
    build(nc, *args)
    r = _run(nc, [arrays], core_ids=[0])
    return r.results[0]["out_0_dram"]
```
